# Optimizing a Trainium2 kernel written in Bass

```python
import numpy as np
import jax
import jax.numpy as jnp

def _softmax(x, axis=-1):
    return jax.nn.softmax(x, axis=axis)

def _gelu(x):
    return jax.nn.gelu(x, approximate=True)

def _silu(x):
    return jax.nn.silu(x)

def _sigmoid(x):
    return jax.nn.sigmoid(x)

def _layernorm(x, axis=-1, eps=1e-05):
    m = jnp.mean(x, axis=axis, keepdims=True)
    v = jnp.var(x, axis=axis, keepdims=True)
    return (x - m) / jnp.sqrt(v + eps)

def _scatter_add(tgt, idx, src, axis=0):
    return tgt.at[idx].add(src)

def _segment_sum(src, seg, n):
    return jax.ops.segment_sum(src, seg, n)
kernel_name = 'mk_conv_preact_d2_conv_nchw256_r2_909901'

def setup_inputs(seed: int=0):
    np.random.seed(seed)
    _w = jnp.asarray

    def _rec_inputs():
        import jax
        import jax.numpy as jnp
        _gk = jax.random.key(seed)
        x = -0.000125 + 0.9999 * jax.random.normal(jax.random.fold_in(_gk, 1), (2, 128, 128, 128), jnp.float32)
        return x
    x = _rec_inputs()

    def _L0_conv_setup():
        import jax, jax.numpy as jnp
        import numpy as np
        DIM = 128
        NUM_HEADS = 16
        WS = 8
        key = jax.random.key(seed)
        ks = jax.random.split(key, 6)
        B, C, H, W = (2, DIM, 128, 128)
        std = 1.0 / np.sqrt(C)
        x = jax.random.normal(ks[0], (B, C, H, W), dtype=jnp.float32)
        ac_w = jax.random.normal(ks[1], (C,), dtype=jnp.float32) * std
        ac_b = jax.random.normal(ks[2], (C,), dtype=jnp.float32) * 0.01
        qkv_w = jax.random.normal(ks[3], (3 * C, C), dtype=jnp.float32) * std
        proj_w = jax.random.normal(ks[4], (C, C), dtype=jnp.float32) * std
        proj_b = jax.random.normal(ks[5], (C,), dtype=jnp.float32) * 0.01
        return {'x': x, 'ac_w': ac_w, 'ac_b': ac_b, 'qkv_w': qkv_w, 'proj_w': proj_w, 'proj_b': proj_b}
    _L0_conv_all = _L0_conv_setup()
    _L0_conv_in = {k: v for k, v in _L0_conv_all.items() if k in ('ac_w', 'ac_b', 'qkv_w', 'proj_w', 'proj_b')}
    del _L0_conv_all

    def _L1_conv_setup():
        import jax, jax.numpy as jnp
        import numpy as np
        key = jax.random.key(seed)
        k1, k2, k3 = jax.random.split(key, 3)
        B, C, H, Wd = (16, 128, 56, 56)
        inp = jax.random.normal(k1, (B, C, H, Wd), dtype=jnp.float32)
        W = jax.random.normal(k2, (C, C, 3, 3), dtype=jnp.float32) / np.sqrt(C * 9)
        bias = jax.random.uniform(k3, (C, 1, 1), dtype=jnp.float32)
        return {'inp': inp, 'W': W, 'bias': bias}
    _L1_conv_all = _L1_conv_setup()
    _L1_conv_in = {k: v for k, v in _L1_conv_all.items() if k in ('W', 'bias')}
    del _L1_conv_all
    return {'x': x, 'L0_conv_ac_w': _L0_conv_in['ac_w'], 'L0_conv_ac_b': _L0_conv_in['ac_b'], 'L0_conv_qkv_w': _L0_conv_in['qkv_w'], 'L0_conv_proj_w': _L0_conv_in['proj_w'], 'L0_conv_proj_b': _L0_conv_in['proj_b'], 'L1_conv_W': _L1_conv_in['W'], 'L1_conv_bias': _L1_conv_in['bias']}

def reference(x, L0_conv_ac_w, L0_conv_ac_b, L0_conv_qkv_w, L0_conv_proj_w, L0_conv_proj_b, L1_conv_W, L1_conv_bias):
    import jax
    import jax.numpy as jnp

    def _L0_conv_ref(x, ac_w, ac_b, qkv_w, proj_w, proj_b):
        import jax, jax.numpy as jnp
        import numpy as np
        DIM = 128
        NUM_HEADS = 16
        WS = 8
        B, C, H, W = x.shape
        N = NUM_HEADS
        hd = C // N
        ws = WS
        scale = hd ** (-0.5)
        nh, nw = (H // ws, W // ws)
        g = (x * ac_w[None, :, None, None] + ac_b[None, :, None, None]) * x
        g = jnp.clip(g, 0.0, 6.0)
        qkv = jnp.einsum('bchw,dc->bdhw', g, qkv_w)
        qkv = qkv.reshape(B, 3, N, hd, nh, ws, nw, ws)
        qkv = qkv.transpose(1, 0, 4, 6, 2, 5, 7, 3).reshape(3, B * nh * nw, N, ws * ws, hd)
        q, k, v = (qkv[0], qkv[1], qkv[2])
        attn = jnp.einsum('wnqd,wnkd->wnqk', q, k) * scale
        attn = jax.nn.softmax(attn, axis=-1)
        o = jnp.einsum('wnqk,wnkd->wnqd', attn, v)
        o = o.reshape(B, nh, nw, N, ws, ws, hd)
        o = o.transpose(0, 3, 6, 1, 4, 2, 5).reshape(B, C, H, W)
        out = jnp.einsum('bchw,dc->bdhw', o, proj_w) + proj_b[None, :, None, None]
        return out

    def _L1_conv_ref(inp, W, bias):
        import jax, jax.numpy as jnp
        import numpy as np
        out = jax.lax.conv_general_dilated(inp, W, window_strides=(1, 1), padding=((1, 1), (1, 1)), dimension_numbers=('NCHW', 'OIHW', 'NCHW'))
        return out + bias[None]

    def _gn(v, G=32, eps=1e-05):
        B_, C_, H_, W_ = v.shape
        g = v.reshape(B_, G, C_ // G, H_, W_)
        m = jnp.mean(g, axis=(2, 3, 4), keepdims=True)
        s = jnp.var(g, axis=(2, 3, 4), keepdims=True)
        return ((g - m) / jnp.sqrt(s + eps)).reshape(v.shape)

    def _ln_c(v, eps=1e-06):
        m = jnp.mean(v, axis=1, keepdims=True)
        s = jnp.var(v, axis=1, keepdims=True)
        return (v - m) / jnp.sqrt(s + eps)

    def _ln_t(v, eps=1e-05):
        m = jnp.mean(v, axis=-1, keepdims=True)
        s = jnp.var(v, axis=-1, keepdims=True)
        return (v - m) / jnp.sqrt(s + eps)

    def _to_tokens(v):
        B_, C_, H_, W_ = v.shape
        return v.reshape(B_, C_, H_ * W_).transpose(0, 2, 1)

    def _from_tokens(t, like):
        B_, C_, H_, W_ = like.shape
        return t.transpose(0, 2, 1).reshape(B_, C_, H_, W_)
    x = x + _L0_conv_ref(_gn(x), L0_conv_ac_w, L0_conv_ac_b, L0_conv_qkv_w, L0_conv_proj_w, L0_conv_proj_b)
    x = x + _L1_conv_ref(_gn(x), L1_conv_W, L1_conv_bias)
    return x

_drawn_inputs = setup_inputs


def setup_inputs(seed=0):
    import zlib

    import numpy as np

    out = dict(_drawn_inputs(seed))
    spreads = {}
    factors = {'L0_conv_ac_b': 40.345, 'L0_conv_proj_b': 5.661}
    for name, (base, spread) in spreads.items():
        noise = np.random.default_rng([zlib.crc32(name.encode()), seed]).standard_normal(out[name].shape)
        drawn = base * np.exp(spread * noise) if base else spread * noise
        out[name] = jnp.asarray(drawn.astype(out[name].dtype))
    for name, factor in factors.items():
        out[name] = (out[name] * factor).astype(out[name].dtype)
    return out
```

```python
from contextlib import ExitStack

import concourse.bass as bass
from concourse import mybir

F32 = mybir.dt.float32
F16 = mybir.dt.float16
ALU = mybir.AluOpType
ACT = mybir.ActivationFunctionType
AX = mybir.AxisListType

P = 128
BATCH = 2
C = 128
SIDE = 128
PIX = SIDE * SIDE
HEADS, HD, WS = 16, 8, 8
WIN = WS * WS
GROUPS, GC = 32, 4
EPS = 1e-5

UW = 8
UT = UW * WIN
UCOL = UW * WS
ACROSS = SIDE // UCOL
UNITS = PIX // UT
HG, HJ = 4, 4
PAIRS = UW // 2
PARTS = 3
ROWS = HJ * HD * PARTS
MROWS = 2 * HJ
HP = HEADS // 2
VC = 4 * HD
BUFS = 3

G_MAX = 6.0
PAIR_MAX = 4096.0
QKV_SCALE = PAIR_MAX / (G_MAX * C)
CONV_SCALE = 256.0
TINY = 1e-12

CROWS = 8
CUNITS = SIDE // CROWS
HALO = CROWS + 2
WIDE = SIDE + 2
TAPS = 9
CHUNK = 4
AHEAD = 4


def build(nc, x, ac_w, ac_b, qkv_w, proj_w, proj_b, conv_w, conv_b, out):
    stackd = nc.dram_tensor("stack_scratch", [BUFS, 2, P, PARTS, UT], F16, kind="Internal").ap()
    maxd = nc.dram_tensor("max_scratch", [BUFS, PAIRS * HEADS, 2, P], F16, kind="Internal").ap()

    ctx = ExitStack()
    with ctx:
        def sb(name, shape, dt=F32):
            return ctx.enter_context(nc.sbuf_tensor(name, shape, dt))

        img = sb("img", [P, SIDE, SIDE])
        q_stack = sb("q_stack", [P, BUFS, HG, UT], F16)
        k_stack = sb("k_stack", [P, BUFS, HG, HJ, UT], F16)
        v_ext = sb("v_ext", [P, BUFS, UW, HP, VC])
        g_hi = sb("g_hi", [P, BUFS, UW, 2, WIN], F16)
        g_lo = sb("g_lo", [P, BUFS, UW, 2, WIN], F16)
        w_hi = sb("w_hi", [P, 3, P], F16)
        w_lo = sb("w_lo", [P, 3, P], F16)
        pw = sb("pw", [P, 2, P])
        c_hi = sb("c_hi", [P, TAPS, P], F16)
        c_lo = sb("c_lo", [P, TAPS, P], F16)
        ident = sb("ident", [P, P])
        share = sb("share", [P, P])
        ones = sb("ones", [2, P])
        vecs = sb("vecs", [P, 4])
        st = sb("st", [P, UNITS, 6])
        sc = sb("sc", [P, 24])
        cf = sb("cf", [P, 12])
        am = sb("am", [P, 8])
        ws = sb("ws", [P, 8])
        m_all = sb("m_all", [P, 2, HG, PAIRS, HJ])
        tick = sb("tick", [P, 1])
        m_pair = sb("m_pair", [PAIRS * HEADS, 2, P], F16)

        work = sb("work", [P, 6912])
        def part(at, n):
            return work[:, at:at + n]
        qk = part(0, 1024).bitcast(F16).rearrange("p (s t) -> p s t", s=4)
        probs = part(1024, 2 * 512).rearrange("p (s t) -> p s t", s=2)
        aff = part(2048, 512)
        gpre = part(2560, 512)
        g32 = part(3072, 512)
        rden = part(3584, 512)
        rsh = part(4096, 512)
        o_n = part(4608, 1024).rearrange("p (w a q) -> p w a q", w=UW, a=2)
        res = part(5632, 512)
        n16 = HALO * WIDE
        cx_hi = [part(i * 652, 650).bitcast(F16).rearrange("p (r c) -> p r c", r=HALO) for i in range(2)]
        cx_lo = [part(1304 + i * 652, 650).bitcast(F16).rearrange("p (r c) -> p r c", r=HALO) for i in range(2)]
        cx32 = part(2608, HALO * SIDE).rearrange("p (r c) -> p r c", r=HALO)
        c_out = [part(4096 + i * 1024, 1024).rearrange("p (r c) -> p r c", r=CROWS) for i in range(2)]
        raw_qkv = part(0, 384).rearrange("p (t c) -> p t c", t=3)
        raw_proj = part(384, 256).rearrange("p (a c r) -> p a c r", a=2, c=4)
        raw_conv = part(640, C * TAPS).rearrange("p (i k) -> p i k", k=TAPS)

        ps = ctx.enter_context(nc.psum_tensor("ps", [P, 8, 512], F32))
        S_B, ST_B, PV_B, GA, GB = 0, 2, 4, 6, 7

        m4 = sb("m4", [P, HJ])
        names = {}
        def sem(name, per=1):
            s = ctx.enter_context(nc.semaphore(name))
            names[name] = (s, per)
            return s

        aff_done = sem("aff_done"); gpre_done = sem("gpre_done"); g32_done = sem("g32_done")
        g_hi_done = sem("g_hi_done", 2); g_lo_done = sem("g_lo_done", 2)
        q_done = sem("q_done"); k_done = sem("k_done"); v_done = sem("v_done", 2)
        q_hi_done = sem("q_hi_done"); q_lo_done = sem("q_lo_done")
        k_hi_done = sem("k_hi_done"); k_lo_done = sem("k_lo_done")
        v_even_done = sem("v_even_done", 2); v_odd_done = sem("v_odd_done", 2)
        qk_sent = sem("qk_sent", 32); stack_in = sem("stack_in", 80)
        s_done = sem("s_done", 8); max_done = sem("max_done", 8)
        mt_done = sem("mt_done"); m_hi_done = sem("m_hi_done"); m_lo_done = sem("m_lo_done")
        m_sent = sem("m_sent", 16); m_in = sem("m_in", 16)
        st_done = sem("st_done", 8); exp_done = sem("exp_done", 8); pv_done = sem("pv_done", 8)
        rden_done = sem("rden_done", 2); rsh_done = sem("rsh_done", 2); o_done = sem("o_done", 2)
        proj_done = sem("proj_done"); res_done = sem("res_done"); x1_done = sem("x1_done")
        bn_done = sem("bn_done")
        chi_done = sem("chi_done"); cx_done = sem("cx_done"); clo_done = sem("clo_done")
        conv_done = sem("conv_done", 2); cev_done = sem("cev_done", 2); cadd_done = sem("cadd_done")
        out_done = sem("out_done", 16); next_in = sem("next_in", 16); nbn_done = sem("nbn_done")
        settled = sem("settled")
        w_in = sem("w_in"); x_in = [sem(f"x_in{i}") for i in range(4)]
        pool_set = sem("pool_set"); pe_step = sem("pe_step"); act_step = sem("act_step")
        dve_step = sem("dve_step"); coef_ready = sem("coef_ready"); pads_zero = sem("pads_zero")
        aggr_done = sem("aggr_done"); gmean_done = sem("gmean_done"); dev_done = sem("dev_done")
        gvar_done = sem("gvar_done"); var_done = sem("var_done"); root_done = sem("root_done")
        amax_done = sem("amax_done"); diag_done = sem("diag_done"); scaled_done = sem("scaled_done")

        COUNTED = [n for n in names if n not in (
            "settled w_in x_in0 x_in1 x_in2 x_in3 pool_set pe_step act_step dve_step coef_ready pads_zero "
            "amax_done diag_done scaled_done aggr_done gmean_done dev_done gvar_done var_done root_done".split())]

        def after(eng, s, unit, k=None):
            name = next(n for n, (h, _) in names.items() if h is s)
            per = names[name][1]
            eng.wait_ge(s, unit * per + (AHEAD * per + (per if k is None else k)))
            if eng is nc.sync:
                eng.sem_inc(settled, 1)

        def pixels(u):
            return (u // ACROSS) * WS, (u % ACROSS) * UCOL

        block = ctx.enter_context(nc.Block())

        def iterations(eng, b, one):
            def active(i):
                return {s for s, lead in (("G", 3), ("B", 2), ("C", 1), ("D", 0), ("R", -1))
                        if 0 <= i + lead < UNITS}
            first, turns = 1, (UNITS - 4) // BUFS
            for i in range(-3, first):
                one(i, i % BUFS, active(i))
            with eng.Fori(0, turns) as t:
                for k in range(BUFS):
                    one(t * BUFS + (first + k), (first + k) % BUFS, active(first))
            for i in range(first + turns * BUFS, UNITS + 1):
                one(i, i % BUFS, active(i))

        def conv_units(eng, b, one):
            one(0, 0, True, False)
            with eng.Fori(0, (CUNITS - 4) // 2) as t:
                one(t * 2 + 1, 1, False, False)
                one(t * 2 + 2, 0, False, False)
            for t in range(CUNITS - 3, CUNITS):
                one(t, t % 2, False, t == CUNITS - 1)

        def key_major(row, by_window=False):
            if by_window:
                return row.rearrange("p (w k) -> p k w", w=UW)
            return row.rearrange("p (k w) -> p k w", w=UW)

        def peeled(i, k):
            return isinstance(i, int) and i == k

        def before_last(t):
            return 1 if peeled(t, CUNITS - 2) else 0

        def v_heads(bank, parity):
            rows = slice(64 * parity, 64 * parity + 64)
            return ps[rows, bank, :].rearrange("p (w h e d) -> p w h e d", w=4, e=2, d=HD)[:, :, :, parity, :]

        A_SLOPE, A_OFF, A_MEAN, C_SLOPE, C_OFF = 0, 1, 2, 3, 4
        S_QKV, S_CONV, R_QKV, R_CONV, R_EXP = 0, 1, 2, 3, 4

        @block.sync
        def _(sp):
            sp.wait_ge(pool_set, 1)
            sp.dma_start(raw_qkv, qkv_w.rearrange("(t d) c -> d t c", t=3)).then_inc(w_in, 16)
            for a in range(2):
                sp.dma_start(raw_proj[:, a, :, 0:2 * HD], proj_w[:, a * 64:(a + 1) * 64].rearrange("o (c r) -> o c r", r=16)).then_inc(w_in, 16)
            sp.dma_start(raw_conv, conv_w.rearrange("o i h w -> o i (h w)")).then_inc(w_in, 16)
            for i, v in enumerate((ac_w, ac_b, proj_b)):
                sp.dma_start(vecs[:, i:i + 1], v.rearrange("(c a) -> c a", a=1)).then_inc(w_in, 16)
            sp.dma_start(vecs[:, 3:4], conv_b.rearrange("c a b -> c (a b)")).then_inc(w_in, 16)
            for i in range(4):
                sp.dma_start(img[:, 32 * i:32 * i + 32, :], x[0, :, 32 * i:32 * i + 32, :]).then_inc(x_in[i], 16)

            for b in range(BATCH):
                def one(i, m, on):
                    n = i + b * UNITS
                    if "B" in on:
                        d, mb = n + 2, (m + 2) % BUFS
                        after(sp, stack_in, d - 1)
                        for s in (q_lo_done, q_hi_done, k_hi_done, k_lo_done):
                            after(sp, s, d)
                        both = stackd[mb].rearrange("a r s t -> r a s t")
                        sp.dma_start(both[:, :, 0:2, :], qk[:, :, :].rearrange("p (a s) t -> p a s t", s=2)).then_inc(qk_sent, 16)
                        sp.dma_start(both[:, :, 2, :], qk[:, 1:3, :]).then_inc(qk_sent, 16)
                        after(sp, qk_sent, d)
                        after(sp, st_done, d - BUFS)
                        sp.dma_start(q_stack[0:ROWS, mb, :, :],
                                     stackd[mb, 0].rearrange("(g r) s t -> (r s) g t", g=HG)).then_inc(stack_in, 16)
                        k_rows = stackd[mb, 1].rearrange("(g j d) s t -> j (d s) g t", g=HG, j=HJ)
                        for j in range(HJ):
                            n_r = HD * PARTS
                            sp.dma_start(k_stack[n_r * j:n_r * j + n_r, mb, :, j, :], k_rows[j]).then_inc(stack_in, 16)
                    if "C" in on:
                        d, mb = n + 1, (m + 1) % BUFS
                        after(sp, m_in, d - 1)
                        after(sp, m_hi_done, d)
                        after(sp, m_lo_done, d)
                        sp.dma_start(maxd[mb], m_pair[:, :, :]).then_inc(m_sent, 16)
                        after(sp, m_sent, d)
                        after(sp, st_done, d - BUFS)
                        sp.dma_start(q_stack[ROWS:ROWS + MROWS, mb, :, :].rearrange("r g (p t) -> r (g p) t", p=PAIRS),
                                     maxd[mb].rearrange("(a j) s t -> (j s) a t", j=HJ)).then_inc(m_in, 16)
                iterations(sp, b, one)

                def conv_one(t, par, top, bottom):
                    n = t + b * CUNITS
                    row = t * CROWS
                    after(sp, cadd_done, n)
                    after(sp, out_done, n - 1)
                    sp.dma_start(out[b, :, bass.ds(row, CROWS), :], c_out[par][:, :, :]).then_inc(out_done, 16)
                    if b + 1 < BATCH and not top:
                        after(sp, chi_done, n)
                        after(sp, cx_done, n)
                        after(sp, next_in, t - 2)
                        sp.dma_start(img[:, bass.ds(row - CROWS, CROWS), :],
                                     x[b + 1, :, bass.ds(row - CROWS, CROWS), :]).then_inc(next_in, 16)
                        if bottom:
                            after(sp, next_in, t - 1)
                            sp.dma_start(img[:, bass.ds(row, CROWS), :],
                                         x[b + 1, :, bass.ds(row, CROWS), :]).then_inc(next_in, 16)
                conv_units(sp, b, conv_one)
            after(sp, out_done, BATCH * CUNITS - 1)

        @block.gpsimd
        def _(pool):
            g = nc.gpsimd
            g.memset(raw_proj, 0.0).then_inc(pool_set, 1)
            pool.wait_ge(pool_set, 1)
            g.memset(ident[:, :], 0.0).then_inc(pool_set, 1)
            pool.wait_ge(pool_set, 2)
            g.memset(share[:, :], 1.0 / GC).then_inc(pool_set, 1)
            pool.wait_ge(pool_set, 3)
            g.memset(ones[:, :], 1.0).then_inc(pool_set, 1)
            pool.wait_ge(pool_set, 4)
            g.memset(m4[ROWS:P, :], -PAIR_MAX).then_inc(pool_set, 1)
            pool.wait_ge(pool_set, 5)
            g.memset(m_all[:, 1, :, :, :], 0.0).then_inc(pool_set, 1)
            pool.wait_ge(pool_set, 6)
            g.affine_select(out=ident[:, :], in_=ident[:, :], compare_op=ALU.not_equal, fill=1.0,
                            base=0, pattern=[[-1, P]], channel_multiplier=1).then_inc(pool_set, 1)
            pool.wait_ge(pool_set, 7)
            sv = share[:, :].rearrange("p (a c) -> p a c", c=GC)
            g.affine_select(out=sv, in_=sv, compare_op=ALU.is_ge, fill=0.0,
                            base=0, pattern=[[-GC, GROUPS], [0, GC]], channel_multiplier=1).then_inc(pool_set, 1)
            pool.wait_ge(pool_set, 8)
            mv = m4[ROWS:P, :]
            g.affine_select(out=mv, in_=mv, compare_op=ALU.is_ge, fill=0.0,
                            base=0, pattern=[[-2, HJ]], channel_multiplier=1).then_inc(pool_set, 1)
            pool.wait_ge(pool_set, 9)
            g.affine_select(out=sv, in_=sv, compare_op=ALU.is_ge, fill=0.0,
                            base=GC - 1, pattern=[[GC, GROUPS], [0, GC]], channel_multiplier=-1).then_inc(pool_set, 1)
            pool.wait_ge(pool_set, 10)
            g.affine_select(out=mv, in_=mv, compare_op=ALU.is_ge, fill=0.0,
                            base=1, pattern=[[2, HJ]], channel_multiplier=-1).then_inc(pool_set, 1)
            pool.wait_ge(pool_set, 11)
            g.memset(k_stack[:, :, :, :, :].bitcast(F32), 0.0).then_inc(pool_set, 1)
            pool.wait_ge(pool_set, 12)
            g.memset(v_ext[:, :, :, :, :], 0.0).then_inc(pool_set, 1)
            pool.wait_ge(pool_set, 13)
            ve = v_ext[:, :, :, :, :].rearrange("p m w h v -> p (m w h) v")
            g.memset(ve[0:64, :, 2 * HD:3 * HD], 1.0).then_inc(pool_set, 1)
            pool.wait_ge(pool_set, 14)
            g.memset(ve[64:P, :, 3 * HD:4 * HD], 1.0).then_inc(pool_set, 1)
            pool.wait_ge(pool_set, 15)

            for b in range(BATCH):
                def one(i, m, on):
                    n = i + b * UNITS
                    if "R" in on:
                        d = n - 1
                        row, col = pixels(i - 1)
                        here = img[:, bass.ds(row, WS), bass.ds(col, UCOL)]
                        after(pool, res_done, d)
                        g.tensor_tensor(here, here, res.rearrange("p (r c) -> p r c", r=WS), ALU.add).then_inc(x1_done, 1)
                    if "G" in on:
                        d, mb = n + 3, m % BUFS
                        after(pool, g_hi_done, d)
                        for e in range(2):
                            g.tensor_tensor(g_lo[:, mb, :, e, :], g32.rearrange("p (w q) -> p w q", w=UW),
                                            g_hi[:, mb, :, e, :], ALU.subtract).then_inc(g_lo_done, 1)
                iterations(pool, b, one)

                def conv_one(t, par, top, bottom):
                    n = t + b * CUNITS
                    after(pool, cev_done, n)
                    g.tensor_tensor(c_out[par][:, :, :], c_out[par][:, :, :],
                                    img[:, bass.ds(t * CROWS, CROWS), :], ALU.add).then_inc(cadd_done, 1)
                conv_units(pool, b, conv_one)

        @block.scalar
        def _(act):
            a = nc.scalar
            for n in COUNTED:
                s, per = names[n]
                act.sem_inc(s, AHEAD * per)

            def root(k):
                act.wait_ge(var_done, k + 1)
                a.activation(sc[:, 5:6], sc[:, 4:5], ACT.Sqrt).then_inc(root_done, 1)

            act.wait_ge(pe_step, 3)
            a.copy(w_hi[:, :, :], ps[:, 0, 0:3 * P].rearrange("p (t d) -> p t d", t=3)).then_inc(act_step, 1)
            act.wait_ge(pe_step, 4)
            a.copy(pw[:, :, :], ps[:, 1, 0:2 * P].rearrange("p (t d) -> p t d", t=2)).then_inc(act_step, 1)
            for j in range(3):
                k0, k1 = 4 * j, min(4 * j + 4, TAPS)
                act.wait_ge(pe_step, 5 + j)
                a.copy(c_hi[:, k0:k1, :], ps[:, 2 + j, 0:(k1 - k0) * P].rearrange("p (t d) -> p t d", t=k1 - k0)).then_inc(act_step, 1)

            for b in range(BATCH):
                root(2 * b)

                def one(i, m, on):
                    n = i + b * UNITS

                    def exps(w):
                        after(act, st_done, n, w + 1)
                        after(act, pv_done, n, w - 1)
                        a.activation(probs[:, w % 2, :], ps[:, ST_B + w % 2, :], ACT.Exp,
                                     scale=ws[:, R_EXP:R_EXP + 1]).then_inc(exp_done, 1)
                    if "B" in on:
                        after(act, q_done, n + 2)
                        after(act, qk_sent, n + 1)
                        a.copy(qk[:, 1, :], ps[:, GA, :]).then_inc(q_hi_done, 1)
                        after(act, k_done, n + 2)
                        a.copy(key_major(qk[:, 2, :]), key_major(ps[:, GB, :], True)).then_inc(k_hi_done, 1)
                    if "D" in on:
                        exps(0)
                    for h in range(2):
                        if "B" in on:
                            mb = (m + 2) % BUFS
                            after(act, v_done, n + 2, h + 1)
                            after(act, pv_done, n + 2 - BUFS)
                            a.copy(v_ext[0:64, mb, 4 * h:4 * h + 4, :, 0:HD],
                                   v_heads(GA + h, 0)).then_inc(v_even_done, 1)
                        if "D" in on:
                            exps(1 + h)
                    if "D" in on:
                        exps(3)
                    if "R" in on:
                        after(act, proj_done, n - 1)
                        after(act, x1_done, n - 2)
                        a.activation(res.rearrange("p (y n x) -> p n y x", y=WS, n=UW),
                                     ps[:, GB, :].rearrange("p (n y x) -> p n y x", y=WS, n=UW), ACT.Identity,
                                     scale=ws[:, R_QKV:R_QKV + 1], bias=vecs[:, 2:3]).then_inc(res_done, 1)
                    if "D" in on:
                        exps(4)
                    if "G" in on:
                        row, col = pixels(i + 3)
                        if peeled(i, -3):
                            act.wait_ge(coef_ready, 2 * b + 1)
                        after(act, gpre_done, n + 2)
                        a.activation(aff.rearrange("p (r c) -> p r c", r=WS), img[:, bass.ds(row, WS), bass.ds(col, UCOL)],
                                     ACT.Identity, scale=cf[:, A_SLOPE:A_SLOPE + 1], bias=cf[:, A_OFF:A_OFF + 1]).then_inc(aff_done, 1)
                    if "D" in on:
                        exps(5)
                    if "C" in on:
                        after(act, mt_done, n + 1)
                        after(act, m_sent, n)
                        a.mul(m_pair[:, 0, :], ps[0:PAIRS * HEADS, GA, 0:P], 1.0 / PAIR_MAX).then_inc(m_hi_done, 1)
                    if "D" in on:
                        exps(6)
                    if "G" in on:
                        after(act, g32_done, n + 3)
                        after(act, v_done, n)
                        for e in range(2):
                            a.copy(g_hi[:, m % BUFS, :, e, :], g32.rearrange("p (w q) -> p w q", w=UW)).then_inc(g_hi_done, 1)
                    if "D" in on:
                        exps(7)
                iterations(act, b, one)

                root(2 * b + 1)

                def conv_one(t, par, top, bottom):
                    n = t + b * CUNITS
                    def high(t, n, par, r0, r1):
                        after(act, conv_done, n - 2)
                        a.activation(cx_hi[par][:, r0:r1, 1:1 + SIDE], img[:, bass.ds(t * CROWS - 1 + r0, r1 - r0), :],
                                     ACT.Identity, scale=cf[:, C_SLOPE:C_SLOPE + 1], bias=cf[:, C_OFF:C_OFF + 1]).then_inc(chi_done, 1)
                    if top:
                        act.wait_ge(coef_ready, 2 * b + 2)
                        high(t, n, par, 1, HALO)
                    if not bottom:
                        high(t + 1, n + 1, 1 - par, 0, HALO - before_last(t))
                    for c in range(2):
                        after(act, conv_done, n, c + 1)
                        after(act, out_done, n - 2)
                        a.activation(c_out[par][:, CHUNK * c:CHUNK * c + CHUNK, :],
                                     ps[:, 2 * par + c, :].rearrange("p (r c) -> p r c", r=CHUNK), ACT.Identity,
                                     scale=ws[:, R_CONV:R_CONV + 1], bias=vecs[:, 3:4]).then_inc(cev_done, 1)
                conv_units(act, b, conv_one)

        @block.vector
        def _(dve):
            v = nc.vector
            chain = [0]

            def link(ins):
                chain[0] += 1
                ins.then_inc(dve_step, 1)
                dve.wait_ge(dve_step, chain[0])

            dve.wait_ge(w_in, 16 * 8)
            v.tensor_reduce(am[:, 0:1], raw_qkv, AX.XY, ALU.max, apply_absolute_value=True).then_inc(amax_done, 1)
            v.tensor_reduce(am[:, 1:2], raw_conv, AX.XY, ALU.max, apply_absolute_value=True).then_inc(amax_done, 1)
            dve.wait_ge(pe_step, 1)
            link(v.tensor_reduce(am[0:2, 2:3], ps[0:2, 0, 0:P], AX.X, ALU.max))
            dve.wait_ge(pool_set, 7)
            v.tensor_scalar(am[0:2, 4:6], ident[0:2, 0:2], am[0:2, 2:3], None, ALU.mult).then_inc(diag_done, 1)
            dve.wait_ge(pe_step, 2)
            link(v.tensor_scalar(am[:, 6:8], ps[:, 0, 0:2], TINY, None, ALU.max))
            link(v.reciprocal(ws[:, 6:8], am[:, 6:8]))
            for col, src, f in ((S_QKV, ws[:, 6:7], QKV_SCALE), (S_CONV, ws[:, 7:8], CONV_SCALE),
                                (R_QKV, am[:, 6:7], 1.0 / QKV_SCALE), (R_CONV, am[:, 7:8], 1.0 / CONV_SCALE)):
                link(v.tensor_scalar(ws[:, col:col + 1], src, f, None, ALU.mult))
            link(v.tensor_scalar(ws[:, 5:6], ws[:, R_QKV:R_QKV + 1], HD ** -0.5, None, ALU.mult))
            link(v.tensor_tensor(ws[:, R_EXP:R_EXP + 1], ws[:, 5:6], ws[:, R_QKV:R_QKV + 1], ALU.mult))
            v.tensor_scalar(raw_qkv, raw_qkv, ws[:, S_QKV:S_QKV + 1], None, ALU.mult).then_inc(scaled_done, 1)
            v.tensor_scalar(raw_conv, raw_conv, ws[:, S_CONV:S_CONV + 1], None, ALU.mult).then_inc(scaled_done, 1)

            flat = img[:, :, :].rearrange("p r c -> p (r c)")
            for i in range(UNITS):
                dve.wait_ge(x_in[i // 8], 16)
                last = v.bn_stats(st[:, i, :], flat[:, i * UT:(i + 1) * UT])
            link(last)

            def norm(k):
                mean, var, gm, dev, gv, root, r, t0, t1 = (sc[:, j:j + 1] for j in (0, 1, 2, 3, 4, 5, 6, 7, 8))
                if k:
                    dve.wait_ge(root_done, k)
                v.bn_aggr(sc[:, 0:2], st[:, :, :].rearrange("p u s -> p (u s)")).then_inc(aggr_done, 1)
                dve.wait_ge(gmean_done, k + 1)
                link(v.tensor_copy(gm, ps[:, GA, 0:1]))
                link(v.tensor_tensor(t0, mean, gm, ALU.subtract))
                link(v.tensor_tensor(t1, t0, t0, ALU.mult))
                v.tensor_tensor(dev, t1, var, ALU.add).then_inc(dev_done, 1)
                dve.wait_ge(gvar_done, k + 1)
                v.tensor_scalar(gv, ps[:, GA, 1:2], EPS, None, ALU.add).then_inc(var_done, 1)
                dve.wait_ge(root_done, k + 1)
                link(v.reciprocal(r, root))
                link(v.tensor_tensor(t0, r, r, ALU.mult))
                link(v.tensor_tensor(t1, t0, gv, ALU.mult))
                link(v.tensor_scalar(t0, t1, -0.5, 1.5, ALU.mult, ALU.add))
                link(v.tensor_tensor(t1, r, t0, ALU.mult))
                link(v.tensor_copy(r, t1))
                return gm, r, t0, t1

            for c in range(3):
                if c == 0:
                    dve.wait_ge(act_step, 1)
                    link(v.tensor_tensor(w_lo[:, :, :], ps[:, 0, 0:3 * P].rearrange("p (t d) -> p t d", t=3), w_hi[:, :, :], ALU.subtract))
                k0, k1 = 4 * c, min(4 * c + 4, TAPS)
                dve.wait_ge(act_step, 3 + c)
                link(v.tensor_tensor(c_lo[:, k0:k1, :], ps[:, 2 + c, 0:(k1 - k0) * P].rearrange("p (t d) -> p t d", t=k1 - k0),
                                     c_hi[:, k0:k1, :], ALU.subtract))
            dve.wait_ge(pool_set, 15)
            for j in range(HJ):
                rows = k_stack[ROWS:ROWS + MROWS, :, :, j, :].rearrange("p m g t -> p (m g) t")
                link(v.tensor_scalar(rows, rows, m4[ROWS:ROWS + MROWS, j:j + 1], None, ALU.add))

            for b in range(BATCH):
                gm, r, t0, t1 = norm(2 * b)
                link(v.tensor_tensor(t0, r, vecs[:, 0:1], ALU.mult))
                link(v.tensor_tensor(t1, t0, gm, ALU.mult))
                link(v.tensor_tensor(sc[:, 9:10], vecs[:, 1:2], t1, ALU.subtract))
                link(v.tensor_tensor(cf[:, A_SLOPE:A_SLOPE + 1], t0, r, ALU.mult))
                link(v.tensor_tensor(cf[:, A_OFF:A_OFF + 1], sc[:, 9:10], r, ALU.mult))
                v.tensor_copy(cf[:, A_MEAN:A_MEAN + 1], gm).then_inc(coef_ready, 1)
                dve.wait_ge(coef_ready, 2 * b + 1)

                def one(i, m, on):
                    n = i + b * UNITS

                    def divide(d, h):
                        after(dve, pv_done, d, 4 * h + 4)
                        after(dve, o_done, d, h)
                        v.reciprocal(rden, ps[:, PV_B + h, :]).then_inc(rden_done, 1)
                        after(dve, rden_done, d, h + 1)
                        v.memset(tick[:, :], 0.0)
                        v.stream_shuffle(rsh, rden, [16 + j % 16 for j in range(32)]).then_inc(rsh_done, 1)
                        after(dve, rsh_done, d, h + 1)
                        after(dve, proj_done, d - 1)
                        v.tensor_tensor(o_n[:, 4 * h:4 * h + 4, :, :],
                                        ps[:, PV_B + h, :].rearrange("p (w a q) -> p w a q", w=4, a=2),
                                        rsh.rearrange("p (w a q) -> p w a q", w=4, a=2), ALU.mult).then_inc(o_done, 1)

                    def row_max(p):
                        for h in range(2):
                            after(dve, s_done, n + 1, 2 * p + h + 1)
                            if p == 0 and h == 0:
                                after(dve, mt_done, n)
                            v.tensor_reduce(m_all[:, 0, 2 * h:2 * h + 2, p, :],
                                            ps[:, S_B + h, :].rearrange("p (g j k) -> p g j k", g=2, k=WIN), AX.X,
                                            ALU.max).then_inc(max_done, 1)
                    if peeled(i, 0) and b:
                        after(dve, out_done, b * CUNITS - 1)
                    if "R" in on:
                        divide(n - 1, 1)
                    if "B" in on:
                        after(dve, q_hi_done, n + 2)
                        v.tensor_tensor(qk[:, 0, :], ps[:, GA, :], qk[:, 1, :], ALU.subtract).then_inc(q_lo_done, 1)
                        after(dve, k_hi_done, n + 2)
                        v.tensor_tensor(key_major(qk[:, 3, :]), key_major(ps[:, GB, :], True), key_major(qk[:, 2, :]),
                                        ALU.subtract).then_inc(k_lo_done, 1)
                    for p in range(PAIRS):
                        if "C" in on:
                            row_max(p)
                        if "B" in on and p < 2:
                            after(dve, v_done, n + 2, p + 1)
                            after(dve, pv_done, n + 2 - BUFS)
                            v.tensor_copy(v_ext[64:P, (m + 2) % BUFS, 4 * p:4 * p + 4, :, HD:2 * HD],
                                          v_heads(GA + p, 1)).then_inc(v_odd_done, 1)
                    if "G" in on:
                        row, col = pixels(i + 3)
                        after(dve, aff_done, n + 3)
                        after(dve, g32_done, n + 2)
                        v.scalar_tensor_tensor(out=gpre.rearrange("p (r c) -> p r c", r=WS),
                                               in0=img[:, bass.ds(row, WS), bass.ds(col, UCOL)],
                                               scalar=cf[:, A_MEAN:A_MEAN + 1],
                                               in1=aff.rearrange("p (r c) -> p r c", r=WS),
                                               op0=ALU.subtract, op1=ALU.mult).then_inc(gpre_done, 1)
                        after(dve, gpre_done, n + 3)
                        after(dve, g_lo_done, n + 2)
                        v.tensor_scalar(g32.rearrange("p (n y x) -> p y n x", n=UW, y=WS),
                                        gpre.rearrange("p (y n x) -> p y n x", y=WS, n=UW),
                                        0.0, G_MAX, ALU.max, ALU.min).then_inc(g32_done, 1)
                    if "D" in on:
                        divide(n, 0)
                    if "C" in on:
                        after(dve, m_hi_done, n + 1)
                        v.scalar_tensor_tensor(out=m_pair[:, 1, :], in0=ps[0:PAIRS * HEADS, GA, 0:P], scalar=1.0 / PAIR_MAX,
                                               in1=m_pair[:, 0, :], op0=ALU.mult, op1=ALU.subtract).then_inc(m_lo_done, 1)
                    if "R" in on:
                        row, col = pixels(i - 1)
                        after(dve, x1_done, n - 1)
                        v.bn_stats(st[:, bass.ds(i - 1, 1), :].rearrange("p a s -> p (a s)"),
                                   img[:, bass.ds(row, WS), bass.ds(col, UCOL)]).then_inc(bn_done, 1)
                iterations(dve, b, one)
                after(dve, bn_done, (b + 1) * UNITS - 1)

                gm, r, t0, t1 = norm(2 * b + 1)
                link(v.tensor_copy(cf[:, C_SLOPE:C_SLOPE + 1], r))
                link(v.tensor_tensor(t0, gm, r, ALU.mult))
                v.tensor_scalar(cf[:, C_OFF:C_OFF + 1], t0, -1.0, None, ALU.mult).then_inc(coef_ready, 1)
                dve.wait_ge(coef_ready, 2 * b + 2)
                for buf in cx_hi + cx_lo:
                    v.memset(buf[:, :, 0:WIDE:WIDE - 1], 0.0).then_inc(pads_zero, 1)
                for buf in (cx_hi[0], cx_lo[0]):
                    v.memset(buf[:, 0, 1:1 + SIDE], 0.0).then_inc(pads_zero, 1)

                def conv_one(t, par, top, bottom):
                    n = t + b * CUNITS

                    def low(t, n, par, r0, r1):
                        rows = cx32[:, r0:r1, :]
                        after(dve, clo_done, n - 1)
                        v.tensor_scalar(rows, img[:, bass.ds(t * CROWS - 1 + r0, r1 - r0), :],
                                        cf[:, C_SLOPE:C_SLOPE + 1], cf[:, C_OFF:C_OFF + 1], ALU.mult, ALU.add).then_inc(cx_done, 1)
                        after(dve, cx_done, n)
                        after(dve, chi_done, n)
                        after(dve, conv_done, n - 2)
                        if r1 < HALO:
                            for buf in (cx_hi[par], cx_lo[par]):
                                v.memset(buf[:, HALO - 1, 1:1 + SIDE], 0.0).then_inc(pads_zero, 1)
                        v.tensor_tensor(cx_lo[par][:, r0:r1, 1:1 + SIDE], rows, cx_hi[par][:, r0:r1, 1:1 + SIDE],
                                        ALU.subtract).then_inc(clo_done, 1)
                    if top:
                        low(t, n, par, 1, HALO)
                    if not bottom:
                        low(t + 1, n + 1, 1 - par, 0, HALO - before_last(t))
                    if b + 1 < BATCH and not top:
                        strip_stats(t - 1)
                        if bottom:
                            strip_stats(t)

                def strip_stats(s):
                    after(dve, next_in, s)
                    for half in range(2):
                        last = v.bn_stats(st[:, bass.ds(s * 2 + half, 1), :].rearrange("p a s -> p (a s)"),
                                          img[:, bass.ds(s * CROWS + half * 4, 4), :])
                    last.then_inc(nbn_done, 1)
                conv_units(dve, b, conv_one)
                if b + 1 < BATCH:
                    after(dve, nbn_done, CUNITS - 1)

        @block.tensor
        def _(pe):
            t_ = nc.tensor
            pe.wait_ge(pool_set, 11)
            pe.wait_ge(amax_done, 2)
            t_.transpose(ps[0:2, 0, 0:P], am[:, 0:2], ident[:, :]).then_inc(pe_step, 1)
            pe.wait_ge(diag_done, 1)
            t_.matmul(ps[:, 0, 0:2], ones[:, :], am[0:2, 4:6], start=True, stop=True).then_inc(pe_step, 1)
            pe.wait_ge(scaled_done, 1)
            for k in range(3):
                mm = t_.transpose(ps[:, 0, k * P:(k + 1) * P], raw_qkv[:, k, :], ident[:, :])
            mm.then_inc(pe_step, 1)
            for k in range(2):
                mm = t_.transpose(ps[:, 1, k * P:(k + 1) * P], raw_proj[:, k, :, :].rearrange("p c r -> p (c r)"), ident[:, :])
            mm.then_inc(pe_step, 1)
            pe.wait_ge(scaled_done, 2)
            for k in range(TAPS):
                mm = t_.transpose(ps[:, 2 + k // 4, (k % 4) * P:(k % 4 + 1) * P], raw_conv[:, :, k], ident[:, :])
                if k % 4 == 3 or k == TAPS - 1:
                    mm.then_inc(pe_step, 1)

            def norm(k):
                pe.wait_ge(aggr_done, k + 1)
                t_.matmul(ps[:, GA, 0:1], share[:, :], sc[:, 0:1], start=True, stop=True).then_inc(gmean_done, 1)
                pe.wait_ge(dev_done, k + 1)
                t_.matmul(ps[:, GA, 1:2], share[:, :], sc[:, 3:4], start=True, stop=True).then_inc(gvar_done, 1)

            def three(o, lhs_hi, lhs_lo, rhs_hi, rhs_lo, first=True, last=True):
                t_.matmul(o, lhs_hi, rhs_hi, start=first, stop=False)
                t_.matmul(o, lhs_lo, rhs_hi, start=False, stop=False)
                return t_.matmul(o, lhs_hi, rhs_lo, start=False, stop=last)

            for b in range(BATCH):
                norm(2 * b)

                def one(i, m, on):
                    n = i + b * UNITS

                    def project(which, bank, event):
                        mb = (m + 2) % BUFS
                        three(ps[:, bank, :], w_hi[:, which, :], w_lo[:, which, :],
                              g_hi[:, mb, :, 0, :], g_lo[:, mb, :, 0, :]).then_inc(event, 1)

                    def v_rows(h):
                        mb = (m + 2) % BUFS
                        bank = GA + h
                        if h == 0:
                            after(pe, q_lo_done, n + 2)
                        else:
                            after(pe, k_lo_done, n + 2)
                        for w in range(4 * h, 4 * h + 4):
                            twice = [g[:, mb, w, :, :].rearrange("p e q -> p (e q)") for g in (g_hi, g_lo)]
                            o = ps[:, bank, (w % 4) * P:(w % 4 + 1) * P]
                            mm = three(o, twice[0], twice[1], w_hi[:, 2, :], w_lo[:, 2, :])
                        mm.then_inc(v_done, 1)

                    def keys(buf, rows, g, j0, j1, w):
                        return k_stack[rows, buf, g, j0:j1, :].rearrange("p j (k n) -> p (j k) n", n=UW)[:, :, w]

                    def scores(p):
                        mb = (m + 1) % BUFS
                        for h in range(2):
                            after(pe, max_done, n + 1, 2 * p + h - 1)
                            for gg in range(2):
                                for w in range(2):
                                    win = 2 * p + w
                                    tok = slice(win * WIN, (win + 1) * WIN)
                                    mm = t_.matmul(ps[64 * w:64 * w + 64, S_B + h, gg * 256:gg * 256 + 256],
                                                   q_stack[0:ROWS, mb, 2 * h + gg, tok],
                                                   keys(mb, slice(0, ROWS), 2 * h + gg, 0, HJ, win), start=True, stop=True)
                            mm.then_inc(s_done, 1)

                    def scores_t(w):
                        tok = slice(w * WIN, (w + 1) * WIN)
                        after(pe, exp_done, n, w - 1)
                        for hp in range(HP):
                            g, j = hp // 2, 2 * (hp % 2)
                            mm = t_.matmul(ps[:, ST_B + w % 2, hp * WIN:(hp + 1) * WIN],
                                           keys(m, slice(0, ROWS + MROWS), g, j, j + 2, w),
                                           q_stack[0:ROWS + MROWS, m, g, tok], start=True, stop=True)
                        mm.then_inc(st_done, 1)

                    def weigh(w):
                        after(pe, exp_done, n, w + 1)
                        if w % 4 == 0:
                            after(pe, o_done, n - 1, w // 4 + 1)
                        for hp in range(HP):
                            a, c = hp // 4, hp % 4
                            col = (w % 4) * P + a * WIN
                            mm = t_.matmul(ps[32 * c:32 * c + 32, PV_B + w // 4, col:col + WIN],
                                           v_ext[:, m, w, hp, :], probs[:, w % 2, hp * WIN:(hp + 1) * WIN],
                                           start=True, stop=True)
                        mm.then_inc(pv_done, 1)

                    def output(d):
                        after(pe, o_done, d)
                        for a in range(2):
                            mm = t_.matmul(ps[:, GB, :], pw[:, a, :], o_n[:, :, a, :], start=(a == 0), stop=(a == 1))
                        mm.then_inc(proj_done, 1)

                    if "B" in on:
                        after(pe, g_hi_done, n + 2)
                        after(pe, g_lo_done, n + 2)
                        after(pe, m_lo_done, n)
                        project(0, GA, q_done)
                        after(pe, res_done, n - 2)
                        project(1, GB, k_done)
                    for w in range(UW):
                        if "C" in on and w < PAIRS:
                            if w == 0:
                                after(pe, stack_in, n + 1)
                            scores(w)
                        if "D" in on:
                            if w == 0:
                                after(pe, m_in, n)
                            scores_t(w)
                            if w > 0:
                                weigh(w - 1)
                        if "B" in on and w < 2:
                            v_rows(w)
                        if "R" in on and w == 2:
                            if "B" in on:
                                after(pe, v_even_done, n + 2)
                                after(pe, v_odd_done, n + 2)
                            output(n - 1)
                        if "C" in on and w == 4:
                            after(pe, max_done, n + 1)
                            if "B" in on:
                                after(pe, v_even_done, n + 2, 1)
                                after(pe, v_odd_done, n + 2, 1)
                            t_.transpose(ps[:, GA, 0:P], m_all[:, :, :, :, :].rearrange("p e g a j -> p (e g a j)"),
                                         ident[:, :]).then_inc(mt_done, 1)
                    if "D" in on:
                        weigh(UW - 1)
                iterations(pe, b, one)

                norm(2 * b + 1)

                def conv_one(t, par, top, bottom):
                    n = t + b * CUNITS
                    after(pe, chi_done, n)
                    after(pe, clo_done, n)
                    if top:
                        pe.wait_ge(pads_zero, 8 * b + 6)
                    if bottom:
                        pe.wait_ge(pads_zero, 8 * b + 8)
                    for c in range(2):
                        after(pe, cev_done, n - 2, c + 1)
                        for k in range(TAPS):
                            rows = slice(CHUNK * c + k // 3, CHUNK * c + k // 3 + CHUNK)
                            cols = slice(k % 3, k % 3 + SIDE)
                            mm = three(ps[:, 2 * par + c, :], c_hi[:, k, :], c_lo[:, k, :],
                                       cx_hi[par][:, rows, cols], cx_lo[par][:, rows, cols],
                                       first=(k == 0), last=(k == TAPS - 1))
                        mm.then_inc(conv_done, 1)
                conv_units(pe, b, conv_one)


_INS = ["x", "L0_conv_ac_w", "L0_conv_ac_b", "L0_conv_qkv_w", "L0_conv_proj_w", "L0_conv_proj_b",
        "L1_conv_W", "L1_conv_bias"]
_OUT = ((2, 128, 128, 128), "float32")


def kernel(**inputs):
    import numpy as _np
    import concourse.bacc as _bacc
    from concourse import mybir as _mybir
    from concourse.bass_utils import run_bass_kernel_spmd as _run

    nc = _bacc.Bacc("TRN2", target_bir_lowering=False, num_devices=1)
    arrays, args = {}, []
    for name in _INS:
        a = _np.ascontiguousarray(inputs[name])
        arrays[f"in_{name}_dram"] = a
        args.append(nc.dram_tensor(f"in_{name}_dram", a.shape, _mybir.dt.from_np(a.dtype), kind="ExternalInput").ap())
    shape, dtype = _OUT
    args.append(nc.dram_tensor("out_0_dram", shape, _mybir.dt.from_np(_np.dtype(dtype)), kind="ExternalOutput").ap())
    build(nc, *args)
    r = _run(nc, [arrays], core_ids=[0])
    return r.results[0]["out_0_dram"]
```

```python
from contextlib import ExitStack

import concourse.bass as bass
from concourse import mybir

F32 = mybir.dt.float32
F16 = mybir.dt.float16
ALU = mybir.AluOpType
ACT = mybir.ActivationFunctionType
AX = mybir.AxisListType

P = 128
BATCH = 2
C = 128
SIDE = 128
PIX = SIDE * SIDE
HEADS, HD, WS = 16, 8, 8
WIN = WS * WS
GROUPS, GC = 32, 4
EPS = 1e-5

UW = 8
UT = UW * WIN
UCOL = UW * WS
ACROSS = SIDE // UCOL
UNITS = PIX // UT
HG, HJ = 4, 4
PAIRS = UW // 2
PARTS = 3
ROWS = HJ * HD * PARTS
MROWS = 2 * HJ
HP = HEADS // 2
VC = 4 * HD
BUFS = 3

G_MAX = 6.0
PAIR_MAX = 4096.0
QKV_SCALE = PAIR_MAX / (G_MAX * C)
CONV_SCALE = 256.0
TINY = 1e-12

CROWS = 8
CUNITS = SIDE // CROWS
HALO = CROWS + 2
WIDE = SIDE + 2
TAPS = 9
CHUNK = 4
AHEAD = 4


def build(nc, x, ac_w, ac_b, qkv_w, proj_w, proj_b, conv_w, conv_b, out):
    stackd = nc.dram_tensor("stack_scratch", [BUFS, 2, P, PARTS, UT], F16, kind="Internal").ap()
    maxd = nc.dram_tensor("max_scratch", [BUFS, PAIRS * HEADS, 2, P], F16, kind="Internal").ap()
    zerod = nc.dram_tensor("zero_scratch", [MROWS, HG, UT], F16, kind="Internal").ap()

    ctx = ExitStack()
    with ctx:
        def sb(name, shape, dt=F32):
            return ctx.enter_context(nc.sbuf_tensor(name, shape, dt))

        img = sb("img", [P, SIDE, SIDE])
        q_stack = sb("q_stack", [P, BUFS, HG, UT], F16)
        k_stack = sb("k_stack", [P, BUFS, HG, HJ, UT], F16)
        v_ext = sb("v_ext", [P, BUFS, UW, HP, VC])
        g_hi = sb("g_hi", [P, BUFS, UW, 2, WIN], F16)
        g_lo = sb("g_lo", [P, BUFS, UW, 2, WIN], F16)
        w_hi = sb("w_hi", [P, 3, P], F16)
        w_lo = sb("w_lo", [P, 3, P], F16)
        pw = sb("pw", [P, 2, P])
        c_hi = sb("c_hi", [P, TAPS, P], F16)
        c_lo = sb("c_lo", [P, TAPS, P], F16)
        ident = sb("ident", [P, P])
        share = sb("share", [P, P])
        ones = sb("ones", [2, P])
        vecs = sb("vecs", [P, 4])
        st = sb("st", [P, UNITS, 6])
        sc = sb("sc", [P, 24])
        cf = sb("cf", [P, 12])
        am = sb("am", [P, 8])
        ws = sb("ws", [P, 8])
        m_all = sb("m_all", [P, 2, HG, PAIRS, HJ])
        m_pair = sb("m_pair", [PAIRS * HEADS, 2, P], F16)

        work = sb("work", [P, 8192])
        def part(at, n):
            return work[:, at:at + n]
        qk = part(0, 1024).bitcast(F16).rearrange("p (s t) -> p s t", s=4)
        probs = part(1024, 2 * 512).rearrange("p (s t) -> p s t", s=2)
        aff = part(2048, 512)
        gpre = part(2560, 512)
        g32 = part(3072, 512)
        sums = [part(3584, 512), part(6656, 512)]
        guess = [part(4096, 512), part(7168, 512)]
        recip = [part(6144, 512), part(7680, 512)]
        o_n = part(4608, 1024).rearrange("p (w a q) -> p w a q", w=UW, a=2)
        res = part(5632, 512)
        cx_hi = [part(i * 652, 650).bitcast(F16).rearrange("p (r c) -> p r c", r=HALO) for i in range(2)]
        cx_lo = [part(1304 + i * 652, 650).bitcast(F16).rearrange("p (r c) -> p r c", r=HALO) for i in range(2)]
        cx32 = part(2608, HALO * SIDE).rearrange("p (r c) -> p r c", r=HALO)
        c_out = [part(4096 + i * 1024, 1024).rearrange("p (r c) -> p r c", r=CROWS) for i in range(2)]
        raw_qkv = part(0, 384).rearrange("p (t c) -> p t c", t=3)
        raw_proj = part(384, 256).rearrange("p (a c r) -> p a c r", a=2, c=4)
        raw_conv = part(640, C * TAPS).rearrange("p (i k) -> p i k", k=TAPS)

        ps = ctx.enter_context(nc.psum_tensor("ps", [P, 8, 512], F32))
        S_B, ST_B, PV_B, GA, GB = 0, 2, 4, 6, 7

        m4 = sb("m4", [P, HJ])
        names = {}
        def sem(name, per=1):
            s = ctx.enter_context(nc.semaphore(name))
            names[name] = (s, per)
            return s

        aff_done = sem("aff_done"); gpre_done = sem("gpre_done"); g32_done = sem("g32_done")
        g_hi_done = sem("g_hi_done", 2); g_lo_done = sem("g_lo_done", 2)
        q_done = sem("q_done"); k_done = sem("k_done"); v_done = sem("v_done", 2)
        q_hi_done = sem("q_hi_done"); q_lo_done = sem("q_lo_done")
        k_hi_done = sem("k_hi_done"); k_lo_done = sem("k_lo_done")
        v_out = sem("v_out", 4)
        qk_sent = sem("qk_sent", 32); stack_in = sem("stack_in", 96)
        s_done = sem("s_done", 8); max_done = sem("max_done", 8)
        mt_done = sem("mt_done"); m_hi_done = sem("m_hi_done"); m_lo_done = sem("m_lo_done")
        m_sent = sem("m_sent", 16); m_in = sem("m_in", 16)
        st_done = sem("st_done", 8); exp_done = sem("exp_done", 8); pv_done = sem("pv_done", 8)
        sums_done = sem("sums_done", 2); ln_done = sem("ln_done", 2); guess_done = sem("guess_done", 2)
        near_done = sem("near_done", 2); recip_done = sem("recip_done", 2); o_done = sem("o_done", 2)
        proj_done = sem("proj_done"); res_done = sem("res_done"); x1_done = sem("x1_done")
        bn_done = sem("bn_done")
        chi_done = sem("chi_done"); cx_done = sem("cx_done"); clo_done = sem("clo_done")
        conv_done = sem("conv_done", 2); cev_done = sem("cev_done", 2); cadd_done = sem("cadd_done")
        out_done = sem("out_done", 16); next_in = sem("next_in", 16); nbn_done = sem("nbn_done")
        settled = sem("settled")
        zeros_out = sem("zeros_out"); w_in = sem("w_in"); x_in = [sem(f"x_in{i}") for i in range(4)]
        pool_set = sem("pool_set"); pe_step = sem("pe_step"); act_step = sem("act_step")
        dve_step = sem("dve_step"); coef_ready = sem("coef_ready"); pads_zero = sem("pads_zero")
        aggr_done = sem("aggr_done"); gmean_done = sem("gmean_done"); dev_done = sem("dev_done")
        gvar_done = sem("gvar_done"); var_done = sem("var_done"); root_done = sem("root_done")
        amax_done = sem("amax_done"); diag_done = sem("diag_done"); scaled_done = sem("scaled_done")

        COUNTED = [n for n in names if n not in (
            "settled zeros_out w_in x_in0 x_in1 x_in2 x_in3 pool_set pe_step act_step dve_step coef_ready pads_zero "
            "amax_done diag_done scaled_done aggr_done gmean_done dev_done gvar_done var_done root_done".split())]

        def after(eng, s, unit, k=None):
            name = next(n for n, (h, _) in names.items() if h is s)
            per = names[name][1]
            eng.wait_ge(s, unit * per + (AHEAD * per + (per if k is None else k)))
            if eng is nc.sync:
                settle(eng)

        def settle(eng):
            eng.sem_inc(settled, 1)

        def pixels(u):
            return (u // ACROSS) * WS, (u % ACROSS) * UCOL

        block = ctx.enter_context(nc.Block())

        def iterations(eng, b, one):
            def active(i):
                return {s for s, lead in (("G", 4), ("H", 3), ("B", 2), ("C", 1), ("D", 0), ("R", -1), ("X", -2))
                        if 0 <= i + lead < UNITS}
            first, turns = 2, (UNITS - 6) // BUFS
            for i in range(-4, first):
                one(i, i % BUFS, active(i))
            with eng.Fori(0, turns) as t:
                for k in range(BUFS):
                    one(t * BUFS + (first + k), (first + k) % BUFS, active(first))
            for i in range(first + turns * BUFS, UNITS + 2):
                one(i, i % BUFS, active(i))

        def conv_units(eng, b, one):
            one(0, 0, True, False)
            with eng.Fori(0, (CUNITS - 4) // 2) as t:
                one(t * 2 + 1, 1, False, False)
                one(t * 2 + 2, 0, False, False)
            for t in range(CUNITS - 3, CUNITS):
                one(t, t % 2, False, t == CUNITS - 1)

        def key_major(row, by_window=False):
            if by_window:
                return row.rearrange("p (w k) -> p k w", w=UW)
            return row.rearrange("p (k w) -> p k w", w=UW)

        def peeled(i, k):
            return isinstance(i, int) and i == k

        def before_last(t):
            return 1 if peeled(t, CUNITS - 2) else 0

        def v_heads(bank, parity):
            rows = slice(64 * parity, 64 * parity + 64)
            return ps[rows, bank, :].rearrange("p (w h e d) -> p w h e d", w=4, e=2, d=HD)[:, :, :, parity, :]

        A_SLOPE, A_OFF, A_MEAN, C_SLOPE, C_OFF = 0, 1, 2, 3, 4
        S_QKV, S_CONV, R_QKV, R_CONV, R_EXP, R_RES = 0, 1, 2, 3, 4, 5

        @block.sync
        def _(sp):
            sp.wait_ge(pool_set, 1)
            sp.dma_start(raw_qkv, qkv_w.rearrange("(t d) c -> d t c", t=3)).then_inc(w_in, 16)
            for a in range(2):
                sp.dma_start(raw_proj[:, a, :, 0:2 * HD], proj_w[:, a * 64:(a + 1) * 64].rearrange("o (c r) -> o c r", r=16)).then_inc(w_in, 16)
            sp.dma_start(raw_conv, conv_w.rearrange("o i h w -> o i (h w)")).then_inc(w_in, 16)
            for i, v in enumerate((ac_w, ac_b, proj_b)):
                sp.dma_start(vecs[:, i:i + 1], v.rearrange("(c a) -> c a", a=1)).then_inc(w_in, 16)
            sp.dma_start(vecs[:, 3:4], conv_b.rearrange("c a b -> c (a b)")).then_inc(w_in, 16)
            for i in range(4):
                sp.dma_start(img[:, 32 * i:32 * i + 32, :], x[0, :, 32 * i:32 * i + 32, :]).then_inc(x_in[i], 16)
            sp.wait_ge(pool_set, 12)
            sp.dma_start(zerod, k_stack[0:MROWS, 0, :, 0, :]).then_inc(zeros_out, 16)
            sp.wait_ge(zeros_out, 16)

            for b in range(BATCH):
                def one(i, m, on):
                    n = i + b * UNITS
                    if "B" in on:
                        d, mb = n + 2, (m + 2) % BUFS
                        after(sp, stack_in, d - 1)
                        for s in (q_lo_done, q_hi_done, k_hi_done, k_lo_done):
                            after(sp, s, d)
                        both = stackd[mb].rearrange("a r s t -> r a s t")
                        sp.dma_start(both[:, :, 0:2, :], qk[:, :, :].rearrange("p (a s) t -> p a s t", s=2)).then_inc(qk_sent, 16)
                        sp.dma_start(both[:, :, 2, :], qk[:, 1:3, :]).then_inc(qk_sent, 16)
                        after(sp, qk_sent, d)
                        after(sp, st_done, d - BUFS)
                        sp.dma_start(q_stack[0:ROWS, mb, :, :],
                                     stackd[mb, 0].rearrange("(g r) s t -> (r s) g t", g=HG)).then_inc(stack_in, 16)
                        sp.dma_start(q_stack[ROWS:ROWS + MROWS, mb, :, :], zerod).then_inc(stack_in, 16)
                        k_rows = stackd[mb, 1].rearrange("(g j d) s t -> j (d s) g t", g=HG, j=HJ)
                        for j in range(HJ):
                            n_r = HD * PARTS
                            sp.dma_start(k_stack[n_r * j:n_r * j + n_r, mb, :, j, :], k_rows[j]).then_inc(stack_in, 16)
                    if "C" in on:
                        d, mb = n + 1, (m + 1) % BUFS
                        after(sp, m_in, d - 1)
                        after(sp, m_hi_done, d)
                        after(sp, m_lo_done, d)
                        sp.dma_start(maxd[mb], m_pair[:, :, :]).then_inc(m_sent, 16)
                        after(sp, m_sent, d)
                        after(sp, st_done, d - BUFS)
                        sp.dma_start(q_stack[ROWS:ROWS + MROWS, mb, :, :].rearrange("r g (p t) -> r (g p) t", p=PAIRS),
                                     maxd[mb].rearrange("(a j) s t -> (j s) a t", j=HJ)).then_inc(m_in, 16)
                iterations(sp, b, one)

                def conv_one(t, par, top, bottom):
                    n = t + b * CUNITS
                    row = t * CROWS
                    after(sp, cadd_done, n)
                    after(sp, out_done, n - 1)
                    sp.dma_start(out[b, :, bass.ds(row, CROWS), :], c_out[par][:, :, :]).then_inc(out_done, 16)
                    if b + 1 < BATCH and not top:
                        after(sp, chi_done, n)
                        after(sp, cx_done, n)
                        after(sp, next_in, t - 2)
                        sp.dma_start(img[:, bass.ds(row - CROWS, CROWS), :],
                                     x[b + 1, :, bass.ds(row - CROWS, CROWS), :]).then_inc(next_in, 16)
                        if bottom:
                            after(sp, next_in, t - 1)
                            sp.dma_start(img[:, bass.ds(row, CROWS), :],
                                         x[b + 1, :, bass.ds(row, CROWS), :]).then_inc(next_in, 16)
                conv_units(sp, b, conv_one)
            after(sp, out_done, BATCH * CUNITS - 1)

        @block.gpsimd
        def _(pool):
            g = nc.gpsimd
            g.memset(raw_proj, 0.0).then_inc(pool_set, 1)
            pool.wait_ge(pool_set, 1)
            g.memset(ident[:, :], 0.0).then_inc(pool_set, 1)
            pool.wait_ge(pool_set, 2)
            g.memset(share[:, :], 1.0 / GC).then_inc(pool_set, 1)
            pool.wait_ge(pool_set, 3)
            g.memset(ones[:, :], 1.0).then_inc(pool_set, 1)
            pool.wait_ge(pool_set, 4)
            g.memset(m4[ROWS:P, :], -PAIR_MAX).then_inc(pool_set, 1)
            pool.wait_ge(pool_set, 5)
            g.memset(m_all[:, 1, :, :, :], 0.0).then_inc(pool_set, 1)
            pool.wait_ge(pool_set, 6)
            g.affine_select(out=ident[:, :], in_=ident[:, :], compare_op=ALU.not_equal, fill=1.0,
                            base=0, pattern=[[-1, P]], channel_multiplier=1).then_inc(pool_set, 1)
            pool.wait_ge(pool_set, 7)
            sv = share[:, :].rearrange("p (a c) -> p a c", c=GC)
            g.affine_select(out=sv, in_=sv, compare_op=ALU.is_ge, fill=0.0,
                            base=0, pattern=[[-GC, GROUPS], [0, GC]], channel_multiplier=1).then_inc(pool_set, 1)
            pool.wait_ge(pool_set, 8)
            mv = m4[ROWS:P, :]
            g.affine_select(out=mv, in_=mv, compare_op=ALU.is_ge, fill=0.0,
                            base=0, pattern=[[-2, HJ]], channel_multiplier=1).then_inc(pool_set, 1)
            pool.wait_ge(pool_set, 9)
            g.affine_select(out=sv, in_=sv, compare_op=ALU.is_ge, fill=0.0,
                            base=GC - 1, pattern=[[GC, GROUPS], [0, GC]], channel_multiplier=-1).then_inc(pool_set, 1)
            pool.wait_ge(pool_set, 10)
            g.affine_select(out=mv, in_=mv, compare_op=ALU.is_ge, fill=0.0,
                            base=1, pattern=[[2, HJ]], channel_multiplier=-1).then_inc(pool_set, 1)
            pool.wait_ge(pool_set, 11)
            g.memset(k_stack[:, :, :, :, :].bitcast(F32), 0.0).then_inc(pool_set, 1)
            pool.wait_ge(pool_set, 12)
            g.memset(v_ext[:, :, :, :, :], 0.0).then_inc(pool_set, 1)
            pool.wait_ge(pool_set, 13)
            g.memset(q_stack[ROWS:P, :, :, :], 0.0).then_inc(pool_set, 1)
            pool.wait_ge(pool_set, 14)
            ve = v_ext[:, :, :, :, :].rearrange("p m w h v -> p (m w h) v")
            g.memset(ve[0:64, :, 2 * HD:3 * HD], 1.0).then_inc(pool_set, 1)
            pool.wait_ge(pool_set, 15)
            g.memset(ve[64:P, :, 3 * HD:4 * HD], 1.0).then_inc(pool_set, 1)
            pool.wait_ge(pool_set, 16)

            for b in range(BATCH):
                def one(i, m, on):
                    n = i + b * UNITS

                    def nearness(d, h):
                        after(pool, guess_done, d, h + 1)
                        after(pool, o_done, d - 1, h + 1)
                        g.tensor_tensor(recip[h], sums[h], guess[h], ALU.mult).then_inc(near_done, 1)
                    if "R" in on:
                        nearness(n - 1, 1)
                    if "H" in on:
                        after(pool, g_hi_done, n + 3)
                        for e in range(2):
                            g.tensor_tensor(g_lo[:, m, :, e, :], g32.rearrange("p (w q) -> p w q", w=UW),
                                            g_hi[:, m, :, e, :], ALU.subtract).then_inc(g_lo_done, 1)
                    if "D" in on:
                        nearness(n, 0)
                    if "R" in on:
                        row, col = pixels(i - 1)
                        here = img[:, bass.ds(row, WS), bass.ds(col, UCOL)]
                        after(pool, res_done, n - 1)
                        g.tensor_tensor(here, here, res.rearrange("p (r c) -> p r c", r=WS), ALU.add).then_inc(x1_done, 1)
                iterations(pool, b, one)

                def conv_one(t, par, top, bottom):
                    n = t + b * CUNITS
                    after(pool, cev_done, n)
                    g.tensor_tensor(c_out[par][:, :, :], c_out[par][:, :, :],
                                    img[:, bass.ds(t * CROWS, CROWS), :], ALU.add).then_inc(cadd_done, 1)
                conv_units(pool, b, conv_one)

        @block.scalar
        def _(act):
            a = nc.scalar
            for n in COUNTED:
                s, per = names[n]
                act.sem_inc(s, AHEAD * per)

            def root(k):
                act.wait_ge(var_done, k + 1)
                a.activation(sc[:, 5:6], sc[:, 4:5], ACT.Sqrt).then_inc(root_done, 1)

            act.wait_ge(pe_step, 3)
            a.copy(w_hi[:, :, :], ps[:, 0, 0:3 * P].rearrange("p (t d) -> p t d", t=3)).then_inc(act_step, 1)
            act.wait_ge(pe_step, 4)
            a.copy(pw[:, :, :], ps[:, 1, 0:2 * P].rearrange("p (t d) -> p t d", t=2)).then_inc(act_step, 1)
            for j in range(3):
                k0, k1 = 4 * j, min(4 * j + 4, TAPS)
                act.wait_ge(pe_step, 5 + j)
                a.copy(c_hi[:, k0:k1, :], ps[:, 2 + j, 0:(k1 - k0) * P].rearrange("p (t d) -> p t d", t=k1 - k0)).then_inc(act_step, 1)

            for b in range(BATCH):
                root(2 * b)
                act.preload_act_table_set("natural_log_exp_and_others")

                def one(i, m, on):
                    n = i + b * UNITS

                    def exps(w):
                        after(act, st_done, n, w + 1)
                        after(act, pv_done, n, w - 1)
                        a.activation(probs[:, w % 2, :], ps[:, ST_B + w % 2, :], ACT.Exp,
                                     scale=ws[:, R_EXP:R_EXP + 1]).then_inc(exp_done, 1)

                    def guesses(d, h):
                        after(act, sums_done, d, h + 1)
                        a.activation(guess[h], sums[h], ACT.Ln).then_inc(ln_done, 1)
                        after(act, ln_done, d, h + 1)
                        a.activation(guess[h], guess[h], ACT.Exp, scale=-1.0).then_inc(guess_done, 1)

                    def v_copies(h):
                        mb = (m + 2) % BUFS
                        after(act, v_done, n + 2, h + 1)
                        after(act, pv_done, n + 2 - BUFS)
                        for parity in range(2):
                            a.copy(v_ext[64 * parity:64 * parity + 64, mb, 4 * h:4 * h + 4, :, HD * parity:HD * parity + HD],
                                   v_heads(GA + h, parity)).then_inc(v_out, 1)
                    if "B" in on:
                        after(act, q_done, n + 2)
                        after(act, qk_sent, n + 1)
                        a.copy(qk[:, 1, :], ps[:, GA, :]).then_inc(q_hi_done, 1)
                    if "R" in on:
                        guesses(n - 1, 1)
                    if "B" in on:
                        after(act, k_done, n + 2)
                        a.copy(key_major(qk[:, 2, :]), key_major(ps[:, GB, :], True)).then_inc(k_hi_done, 1)
                    if "D" in on:
                        exps(0)
                        exps(1)
                    if "B" in on:
                        v_copies(0)
                    if "D" in on:
                        exps(2)
                    if "H" in on:
                        after(act, g32_done, n + 3)
                        after(act, v_done, n)
                        for e in range(2):
                            a.copy(g_hi[:, m, :, e, :], g32.rearrange("p (w q) -> p w q", w=UW)).then_inc(g_hi_done, 1)
                    if "D" in on:
                        exps(3)
                    if "B" in on:
                        v_copies(1)
                    if "D" in on:
                        exps(4)
                    if "G" in on:
                        row, col = pixels(i + 4)
                        if peeled(i, -4):
                            act.wait_ge(coef_ready, 2 * b + 1)
                        after(act, gpre_done, n + 3)
                        a.activation(aff.rearrange("p (r c) -> p r c", r=WS), img[:, bass.ds(row, WS), bass.ds(col, UCOL)],
                                     ACT.Identity, scale=cf[:, A_SLOPE:A_SLOPE + 1], bias=cf[:, A_OFF:A_OFF + 1]).then_inc(aff_done, 1)
                    if "D" in on:
                        exps(5)
                        exps(6)
                    if "C" in on:
                        after(act, mt_done, n + 1)
                        after(act, m_sent, n)
                        a.mul(m_pair[:, 0, :], ps[0:PAIRS * HEADS, GA, 0:P], 1.0 / PAIR_MAX).then_inc(m_hi_done, 1)
                    if "D" in on:
                        exps(7)
                        guesses(n, 0)
                    if "R" in on:
                        after(act, proj_done, n - 1)
                        after(act, x1_done, n - 2)
                        a.activation(res.rearrange("p (y n x) -> p n y x", y=WS, n=UW),
                                     ps[:, GB, :].rearrange("p (n y x) -> p n y x", y=WS, n=UW), ACT.Identity,
                                     scale=ws[:, R_RES:R_RES + 1], bias=vecs[:, 2:3]).then_inc(res_done, 1)
                iterations(act, b, one)

                root(2 * b + 1)

                def conv_one(t, par, top, bottom):
                    n = t + b * CUNITS
                    def high(t, n, par, r0, r1):
                        after(act, conv_done, n - 2)
                        a.activation(cx_hi[par][:, r0:r1, 1:1 + SIDE], img[:, bass.ds(t * CROWS - 1 + r0, r1 - r0), :],
                                     ACT.Identity, scale=cf[:, C_SLOPE:C_SLOPE + 1], bias=cf[:, C_OFF:C_OFF + 1]).then_inc(chi_done, 1)
                    if top:
                        act.wait_ge(coef_ready, 2 * b + 2)
                        high(t, n, par, 1, HALO)
                    if not bottom:
                        high(t + 1, n + 1, 1 - par, 0, HALO - before_last(t))
                    for c in range(2):
                        after(act, conv_done, n, c + 1)
                        after(act, out_done, n - 2)
                        a.activation(c_out[par][:, CHUNK * c:CHUNK * c + CHUNK, :],
                                     ps[:, 2 * par + c, :].rearrange("p (r c) -> p r c", r=CHUNK), ACT.Identity,
                                     scale=ws[:, R_CONV:R_CONV + 1], bias=vecs[:, 3:4]).then_inc(cev_done, 1)
                conv_units(act, b, conv_one)

        @block.vector
        def _(dve):
            v = nc.vector
            chain = [0]

            def link(ins):
                chain[0] += 1
                ins.then_inc(dve_step, 1)
                dve.wait_ge(dve_step, chain[0])

            dve.wait_ge(w_in, 16 * 8)
            v.tensor_reduce(am[:, 0:1], raw_qkv, AX.XY, ALU.max, apply_absolute_value=True).then_inc(amax_done, 1)
            v.tensor_reduce(am[:, 1:2], raw_conv, AX.XY, ALU.max, apply_absolute_value=True).then_inc(amax_done, 1)
            dve.wait_ge(pe_step, 1)
            link(v.tensor_reduce(am[0:2, 2:3], ps[0:2, 0, 0:P], AX.X, ALU.max))
            dve.wait_ge(pool_set, 7)
            v.tensor_scalar(am[0:2, 4:6], ident[0:2, 0:2], am[0:2, 2:3], None, ALU.mult).then_inc(diag_done, 1)
            dve.wait_ge(pe_step, 2)
            link(v.tensor_scalar(am[:, 6:8], ps[:, 0, 0:2], TINY, None, ALU.max))
            link(v.reciprocal(ws[:, 6:8], am[:, 6:8]))
            for col, src, f in ((S_QKV, ws[:, 6:7], QKV_SCALE), (S_CONV, ws[:, 7:8], CONV_SCALE),
                                (R_QKV, am[:, 6:7], 1.0 / QKV_SCALE), (R_CONV, am[:, 7:8], 1.0 / CONV_SCALE)):
                link(v.tensor_scalar(ws[:, col:col + 1], src, f, None, ALU.mult))
            link(v.tensor_scalar(ws[:, 5:6], ws[:, R_QKV:R_QKV + 1], HD ** -0.5, None, ALU.mult))
            link(v.tensor_tensor(ws[:, R_EXP:R_EXP + 1], ws[:, 5:6], ws[:, R_QKV:R_QKV + 1], ALU.mult))
            link(v.tensor_scalar(ws[:, R_RES:R_RES + 1], ws[:, R_QKV:R_QKV + 1], -1.0, None, ALU.mult))
            v.tensor_scalar(raw_qkv, raw_qkv, ws[:, S_QKV:S_QKV + 1], None, ALU.mult).then_inc(scaled_done, 1)
            v.tensor_scalar(raw_conv, raw_conv, ws[:, S_CONV:S_CONV + 1], None, ALU.mult).then_inc(scaled_done, 1)

            flat = img[:, :, :].rearrange("p r c -> p (r c)")
            for i in range(UNITS):
                dve.wait_ge(x_in[i // 8], 16)
                last = v.bn_stats(st[:, i, :], flat[:, i * UT:(i + 1) * UT])
            link(last)

            def norm(k):
                mean, var, gm, dev, gv, root, r, t0, t1 = (sc[:, j:j + 1] for j in (0, 1, 2, 3, 4, 5, 6, 7, 8))
                if k:
                    dve.wait_ge(root_done, k)
                v.bn_aggr(sc[:, 0:2], st[:, :, :].rearrange("p u s -> p (u s)")).then_inc(aggr_done, 1)
                dve.wait_ge(gmean_done, k + 1)
                link(v.tensor_copy(gm, ps[:, GA, 0:1]))
                link(v.tensor_tensor(t0, mean, gm, ALU.subtract))
                link(v.tensor_tensor(t1, t0, t0, ALU.mult))
                v.tensor_tensor(dev, t1, var, ALU.add).then_inc(dev_done, 1)
                dve.wait_ge(gvar_done, k + 1)
                v.tensor_scalar(gv, ps[:, GA, 1:2], EPS, None, ALU.add).then_inc(var_done, 1)
                dve.wait_ge(root_done, k + 1)
                link(v.reciprocal(r, root))
                link(v.tensor_tensor(t0, r, r, ALU.mult))
                link(v.tensor_tensor(t1, t0, gv, ALU.mult))
                link(v.tensor_scalar(t0, t1, -0.5, 1.5, ALU.mult, ALU.add))
                link(v.tensor_tensor(t1, r, t0, ALU.mult))
                link(v.tensor_copy(r, t1))
                return gm, r, t0, t1

            for c in range(3):
                if c == 0:
                    dve.wait_ge(act_step, 1)
                    link(v.tensor_tensor(w_lo[:, :, :], ps[:, 0, 0:3 * P].rearrange("p (t d) -> p t d", t=3), w_hi[:, :, :], ALU.subtract))
                k0, k1 = 4 * c, min(4 * c + 4, TAPS)
                dve.wait_ge(act_step, 3 + c)
                link(v.tensor_tensor(c_lo[:, k0:k1, :], ps[:, 2 + c, 0:(k1 - k0) * P].rearrange("p (t d) -> p t d", t=k1 - k0),
                                     c_hi[:, k0:k1, :], ALU.subtract))
            dve.wait_ge(pool_set, 16)
            for j in range(HJ):
                rows = k_stack[ROWS:ROWS + MROWS, :, :, j, :].rearrange("p m g t -> p (m g) t")
                link(v.tensor_scalar(rows, rows, m4[ROWS:ROWS + MROWS, j:j + 1], None, ALU.add))

            for b in range(BATCH):
                gm, r, t0, t1 = norm(2 * b)
                link(v.tensor_tensor(t0, r, vecs[:, 0:1], ALU.mult))
                link(v.tensor_tensor(t1, t0, gm, ALU.mult))
                link(v.tensor_tensor(sc[:, 9:10], vecs[:, 1:2], t1, ALU.subtract))
                link(v.tensor_tensor(cf[:, A_SLOPE:A_SLOPE + 1], t0, r, ALU.mult))
                link(v.tensor_tensor(cf[:, A_OFF:A_OFF + 1], sc[:, 9:10], r, ALU.mult))
                v.tensor_copy(cf[:, A_MEAN:A_MEAN + 1], gm).then_inc(coef_ready, 1)
                dve.wait_ge(coef_ready, 2 * b + 1)

                def one(i, m, on):
                    n = i + b * UNITS

                    def sum_rows(d, h):
                        after(dve, pv_done, d, 4 * h + 4)
                        after(dve, recip_done, d - 1, h + 1)
                        settle(dve)
                        v.stream_shuffle(sums[h], ps[:, PV_B + h, :], [16 + j % 16 for j in range(32)]).then_inc(sums_done, 1)

                    def divide(d, h):
                        after(dve, near_done, d, h + 1)
                        v.scalar_tensor_tensor(out=recip[h], in0=recip[h], scalar=-2.0, in1=guess[h],
                                               op0=ALU.add, op1=ALU.mult).then_inc(recip_done, 1)
                        after(dve, recip_done, d, h + 1)
                        after(dve, proj_done, d - 1)
                        v.tensor_tensor(o_n[:, 4 * h:4 * h + 4, :, :],
                                        ps[:, PV_B + h, :].rearrange("p (w a q) -> p w a q", w=4, a=2),
                                        recip[h].rearrange("p (w a q) -> p w a q", w=4, a=2), ALU.mult).then_inc(o_done, 1)

                    def row_max(p):
                        for h in range(2):
                            after(dve, s_done, n + 1, 2 * p + h + 1)
                            if p == 0 and h == 0:
                                after(dve, mt_done, n)
                            v.tensor_reduce(m_all[:, 0, 2 * h:2 * h + 2, p, :],
                                            ps[:, S_B + h, :].rearrange("p (g j k) -> p g j k", g=2, k=WIN), AX.X,
                                            ALU.max).then_inc(max_done, 1)
                    if peeled(i, 0) and b:
                        after(dve, out_done, b * CUNITS - 1)
                    if "R" in on:
                        sum_rows(n - 1, 1)
                    if "B" in on:
                        after(dve, q_hi_done, n + 2)
                        v.tensor_tensor(qk[:, 0, :], ps[:, GA, :], qk[:, 1, :], ALU.subtract).then_inc(q_lo_done, 1)
                    if "R" in on:
                        divide(n - 1, 0)
                    if "C" in on:
                        row_max(0)
                    if "B" in on:
                        after(dve, k_hi_done, n + 2)
                        v.tensor_tensor(key_major(qk[:, 3, :]), key_major(ps[:, GB, :], True), key_major(qk[:, 2, :]),
                                        ALU.subtract).then_inc(k_lo_done, 1)
                    if "C" in on:
                        row_max(1)
                    if "R" in on:
                        divide(n - 1, 1)
                    if "C" in on:
                        row_max(2)
                        row_max(3)
                    if "X" in on:
                        row, col = pixels(i - 2)
                        after(dve, x1_done, n - 2)
                        v.bn_stats(st[:, bass.ds(i - 2, 1), :].rearrange("p a s -> p (a s)"),
                                   img[:, bass.ds(row, WS), bass.ds(col, UCOL)]).then_inc(bn_done, 1)
                    if "D" in on:
                        sum_rows(n, 0)
                    if "C" in on:
                        after(dve, m_hi_done, n + 1)
                        v.scalar_tensor_tensor(out=m_pair[:, 1, :], in0=ps[0:PAIRS * HEADS, GA, 0:P], scalar=1.0 / PAIR_MAX,
                                               in1=m_pair[:, 0, :], op0=ALU.mult, op1=ALU.subtract).then_inc(m_lo_done, 1)
                    if "G" in on:
                        row, col = pixels(i + 4)
                        after(dve, aff_done, n + 4)
                        after(dve, g32_done, n + 3)
                        v.scalar_tensor_tensor(out=gpre.rearrange("p (r c) -> p r c", r=WS),
                                               in0=img[:, bass.ds(row, WS), bass.ds(col, UCOL)],
                                               scalar=cf[:, A_MEAN:A_MEAN + 1],
                                               in1=aff.rearrange("p (r c) -> p r c", r=WS),
                                               op0=ALU.subtract, op1=ALU.mult).then_inc(gpre_done, 1)
                        after(dve, gpre_done, n + 4)
                        after(dve, g_lo_done, n + 3)
                        v.tensor_scalar(g32.rearrange("p (n y x) -> p y n x", n=UW, y=WS),
                                        gpre.rearrange("p (y n x) -> p y n x", y=WS, n=UW),
                                        0.0, G_MAX, ALU.max, ALU.min).then_inc(g32_done, 1)
                iterations(dve, b, one)
                after(dve, bn_done, (b + 1) * UNITS - 1)

                gm, r, t0, t1 = norm(2 * b + 1)
                link(v.tensor_copy(cf[:, C_SLOPE:C_SLOPE + 1], r))
                link(v.tensor_tensor(t0, gm, r, ALU.mult))
                v.tensor_scalar(cf[:, C_OFF:C_OFF + 1], t0, -1.0, None, ALU.mult).then_inc(coef_ready, 1)
                dve.wait_ge(coef_ready, 2 * b + 2)
                for buf in cx_hi + cx_lo:
                    v.memset(buf[:, :, 0:WIDE:WIDE - 1], 0.0).then_inc(pads_zero, 1)
                for buf in (cx_hi[0], cx_lo[0]):
                    v.memset(buf[:, 0, 1:1 + SIDE], 0.0).then_inc(pads_zero, 1)

                def conv_one(t, par, top, bottom):
                    n = t + b * CUNITS

                    def low(t, n, par, r0, r1):
                        rows = cx32[:, r0:r1, :]
                        after(dve, clo_done, n - 1)
                        v.tensor_scalar(rows, img[:, bass.ds(t * CROWS - 1 + r0, r1 - r0), :],
                                        cf[:, C_SLOPE:C_SLOPE + 1], cf[:, C_OFF:C_OFF + 1], ALU.mult, ALU.add).then_inc(cx_done, 1)
                        after(dve, cx_done, n)
                        after(dve, chi_done, n)
                        after(dve, conv_done, n - 2)
                        if r1 < HALO:
                            for buf in (cx_hi[par], cx_lo[par]):
                                v.memset(buf[:, HALO - 1, 1:1 + SIDE], 0.0).then_inc(pads_zero, 1)
                        v.tensor_tensor(cx_lo[par][:, r0:r1, 1:1 + SIDE], rows, cx_hi[par][:, r0:r1, 1:1 + SIDE],
                                        ALU.subtract).then_inc(clo_done, 1)
                    if top:
                        low(t, n, par, 1, HALO)
                    if not bottom:
                        low(t + 1, n + 1, 1 - par, 0, HALO - before_last(t))
                    if b + 1 < BATCH and not top:
                        strip_stats(t - 1)
                        if bottom:
                            strip_stats(t)

                def strip_stats(s):
                    after(dve, next_in, s)
                    for half in range(2):
                        last = v.bn_stats(st[:, bass.ds(s * 2 + half, 1), :].rearrange("p a s -> p (a s)"),
                                          img[:, bass.ds(s * CROWS + half * 4, 4), :])
                    last.then_inc(nbn_done, 1)
                conv_units(dve, b, conv_one)
                if b + 1 < BATCH:
                    after(dve, nbn_done, CUNITS - 1)

        @block.tensor
        def _(pe):
            t_ = nc.tensor
            pe.wait_ge(pool_set, 11)
            pe.wait_ge(amax_done, 2)
            t_.transpose(ps[0:2, 0, 0:P], am[:, 0:2], ident[:, :]).then_inc(pe_step, 1)
            pe.wait_ge(diag_done, 1)
            t_.matmul(ps[:, 0, 0:2], ones[:, :], am[0:2, 4:6], start=True, stop=True).then_inc(pe_step, 1)
            pe.wait_ge(scaled_done, 1)
            for k in range(3):
                mm = t_.transpose(ps[:, 0, k * P:(k + 1) * P], raw_qkv[:, k, :], ident[:, :])
            mm.then_inc(pe_step, 1)
            for k in range(2):
                mm = t_.transpose(ps[:, 1, k * P:(k + 1) * P], raw_proj[:, k, :, :].rearrange("p c r -> p (c r)"), ident[:, :])
            mm.then_inc(pe_step, 1)
            pe.wait_ge(scaled_done, 2)
            for k in range(TAPS):
                mm = t_.transpose(ps[:, 2 + k // 4, (k % 4) * P:(k % 4 + 1) * P], raw_conv[:, :, k], ident[:, :])
                if k % 4 == 3 or k == TAPS - 1:
                    mm.then_inc(pe_step, 1)

            def norm(k):
                pe.wait_ge(aggr_done, k + 1)
                t_.matmul(ps[:, GA, 0:1], share[:, :], sc[:, 0:1], start=True, stop=True).then_inc(gmean_done, 1)
                pe.wait_ge(dev_done, k + 1)
                t_.matmul(ps[:, GA, 1:2], share[:, :], sc[:, 3:4], start=True, stop=True).then_inc(gvar_done, 1)

            def three(o, lhs_hi, lhs_lo, rhs_hi, rhs_lo, first=True, last=True):
                t_.matmul(o, lhs_hi, rhs_hi, start=first, stop=False)
                t_.matmul(o, lhs_lo, rhs_hi, start=False, stop=False)
                return t_.matmul(o, lhs_hi, rhs_lo, start=False, stop=last)

            for b in range(BATCH):
                norm(2 * b)

                def one(i, m, on):
                    n = i + b * UNITS

                    def project(which, bank, event):
                        mb = (m + 2) % BUFS
                        three(ps[:, bank, :], w_hi[:, which, :], w_lo[:, which, :],
                              g_hi[:, mb, :, 0, :], g_lo[:, mb, :, 0, :]).then_inc(event, 1)

                    def v_rows(h):
                        mb = (m + 2) % BUFS
                        bank = GA + h
                        if h == 0:
                            after(pe, q_lo_done, n + 2)
                        else:
                            after(pe, k_lo_done, n + 2)
                        for w in range(4 * h, 4 * h + 4):
                            twice = [g[:, mb, w, :, :].rearrange("p e q -> p (e q)") for g in (g_hi, g_lo)]
                            o = ps[:, bank, (w % 4) * P:(w % 4 + 1) * P]
                            mm = three(o, twice[0], twice[1], w_hi[:, 2, :], w_lo[:, 2, :])
                        mm.then_inc(v_done, 1)

                    def keys(buf, g, j0, j1, w):
                        return k_stack[:, buf, g, j0:j1, :].rearrange("p j (k n) -> p (j k) n", n=UW)[:, :, w]

                    def scores(p):
                        mb = (m + 1) % BUFS
                        for h in range(2):
                            after(pe, max_done, n + 1, 2 * p + h - 1)
                            for gg in range(2):
                                for w in range(2):
                                    win = 2 * p + w
                                    tok = slice(win * WIN, (win + 1) * WIN)
                                    mm = t_.matmul(ps[64 * w:64 * w + 64, S_B + h, gg * 256:gg * 256 + 256],
                                                   q_stack[:, mb, 2 * h + gg, tok],
                                                   keys(mb, 2 * h + gg, 0, HJ, win), start=True, stop=True)
                            mm.then_inc(s_done, 1)

                    def scores_t(w):
                        tok = slice(w * WIN, (w + 1) * WIN)
                        after(pe, exp_done, n, w - 1)
                        for hp in range(HP):
                            g, j = hp // 2, 2 * (hp % 2)
                            mm = t_.matmul(ps[:, ST_B + w % 2, hp * WIN:(hp + 1) * WIN],
                                           keys(m, g, j, j + 2, w),
                                           q_stack[:, m, g, tok], start=True, stop=True)
                        mm.then_inc(st_done, 1)

                    def weigh(w):
                        after(pe, exp_done, n, w + 1)
                        if w % 4 == 0:
                            after(pe, o_done, n - 1, w // 4 + 1)
                        for hp in range(HP):
                            a, c = hp // 4, hp % 4
                            col = (w % 4) * P + a * WIN
                            mm = t_.matmul(ps[32 * c:32 * c + 32, PV_B + w // 4, col:col + WIN],
                                           v_ext[:, m, w, hp, :], probs[:, w % 2, hp * WIN:(hp + 1) * WIN],
                                           start=True, stop=True)
                        mm.then_inc(pv_done, 1)

                    def output(d):
                        after(pe, o_done, d)
                        for a in range(2):
                            mm = t_.matmul(ps[:, GB, :], pw[:, a, :], o_n[:, :, a, :], start=(a == 0), stop=(a == 1))
                        mm.then_inc(proj_done, 1)

                    if "B" in on:
                        after(pe, g_hi_done, n + 2)
                        after(pe, g_lo_done, n + 2)
                        after(pe, m_lo_done, n)
                        after(pe, v_out, n + 1)
                        project(0, GA, q_done)
                    if "C" in on:
                        after(pe, stack_in, n + 1)
                        scores(0)
                    if "B" in on:
                        after(pe, res_done, n - 2)
                        project(1, GB, k_done)
                        v_rows(0)
                    if "D" in on:
                        after(pe, m_in, n)
                        scores_t(0)
                        scores_t(1)
                        weigh(0)
                    if "C" in on:
                        scores(1)
                    if "D" in on:
                        scores_t(2)
                        weigh(1)
                    if "B" in on:
                        v_rows(1)
                    if "C" in on:
                        scores(2)
                    if "D" in on:
                        scores_t(3)
                        weigh(2)
                        scores_t(4)
                        weigh(3)
                    if "C" in on:
                        scores(3)
                    if "D" in on:
                        scores_t(5)
                        weigh(4)
                        scores_t(6)
                    if "R" in on:
                        if "B" in on:
                            after(pe, v_out, n + 2)
                        output(n - 1)
                    if "D" in on:
                        weigh(5)
                    if "C" in on:
                        after(pe, max_done, n + 1)
                        if "B" in on:
                            after(pe, v_out, n + 2, 2)
                        t_.transpose(ps[:, GA, 0:P], m_all[:, :, :, :, :].rearrange("p e g a j -> p (e g a j)"),
                                     ident[:, :]).then_inc(mt_done, 1)
                    if "D" in on:
                        scores_t(7)
                        weigh(6)
                        weigh(7)
                iterations(pe, b, one)

                norm(2 * b + 1)

                def conv_one(t, par, top, bottom):
                    n = t + b * CUNITS
                    after(pe, chi_done, n)
                    after(pe, clo_done, n)
                    if top:
                        pe.wait_ge(pads_zero, 8 * b + 6)
                    if bottom:
                        pe.wait_ge(pads_zero, 8 * b + 8)
                    for c in range(2):
                        after(pe, cev_done, n - 2, c + 1)
                        for k in range(TAPS):
                            rows = slice(CHUNK * c + k // 3, CHUNK * c + k // 3 + CHUNK)
                            cols = slice(k % 3, k % 3 + SIDE)
                            mm = three(ps[:, 2 * par + c, :], c_hi[:, k, :], c_lo[:, k, :],
                                       cx_hi[par][:, rows, cols], cx_lo[par][:, rows, cols],
                                       first=(k == 0), last=(k == TAPS - 1))
                        mm.then_inc(conv_done, 1)
                conv_units(pe, b, conv_one)


_INS = ["x", "L0_conv_ac_w", "L0_conv_ac_b", "L0_conv_qkv_w", "L0_conv_proj_w", "L0_conv_proj_b",
        "L1_conv_W", "L1_conv_bias"]
_OUT = ((2, 128, 128, 128), "float32")


def kernel(**inputs):
    import numpy as _np
    import concourse.bacc as _bacc
    from concourse import mybir as _mybir
    from concourse.bass_utils import run_bass_kernel_spmd as _run

    nc = _bacc.Bacc("TRN2", target_bir_lowering=False, num_devices=1)
    arrays, args = {}, []
    for name in _INS:
        a = _np.ascontiguousarray(inputs[name])
        arrays[f"in_{name}_dram"] = a
        args.append(nc.dram_tensor(f"in_{name}_dram", a.shape, _mybir.dt.from_np(a.dtype), kind="ExternalInput").ap())
    shape, dtype = _OUT
    args.append(nc.dram_tensor("out_0_dram", shape, _mybir.dt.from_np(_np.dtype(dtype)), kind="ExternalOutput").ap())
    build(nc, *args)
    r = _run(nc, [arrays], core_ids=[0])
    return r.results[0]["out_0_dram"]
```

```python
from contextlib import ExitStack

import concourse.bass as bass
from concourse import mybir

F32 = mybir.dt.float32
F16 = mybir.dt.float16
ALU = mybir.AluOpType
ACT = mybir.ActivationFunctionType
AX = mybir.AxisListType

P = 128
BATCH = 2
C = 128
SIDE = 128
PIX = SIDE * SIDE
HEADS, HD, WS = 16, 8, 8
WIN = WS * WS
GROUPS, GC = 32, 4
EPS = 1e-5

UW = 8
UT = UW * WIN
UCOL = UW * WS
ACROSS = SIDE // UCOL
UNITS = PIX // UT
HG, HJ = 4, 4
PAIRS = UW // 2
PARTS = 3
ROWS = HJ * HD * PARTS
MROWS = 2 * HJ
HP = HEADS // 2
VC = 4 * HD
BUFS = 3

G_MAX = 6.0
PAIR_MAX = 4096.0
QKV_SCALE = PAIR_MAX / (G_MAX * C)
CONV_SCALE = 256.0
TINY = 1e-12

CROWS = 8
CUNITS = SIDE // CROWS
HALO = CROWS + 2
WIDE = SIDE + 2
TAPS = 9
PLANES = 4
ROW_TAPS = 3
MATS = PLANES * ROW_TAPS
LOADS = 8
AHEAD = 4


def build(nc, x, ac_w, ac_b, qkv_w, proj_w, proj_b, conv_w, conv_b, out):
    stackd = nc.dram_tensor("stack_scratch", [BUFS, 2, P, PARTS, UT], F16, kind="Internal").ap()
    maxd = nc.dram_tensor("max_scratch", [BUFS, PAIRS * HEADS, 2, P], F16, kind="Internal").ap()
    zerod = nc.dram_tensor("zero_scratch", [MROWS, HG, UT], F16, kind="Internal").ap()

    ctx = ExitStack()
    with ctx:
        def sb(name, shape, dt=F32):
            return ctx.enter_context(nc.sbuf_tensor(name, shape, dt))

        img = sb("img", [P, SIDE, SIDE])
        q_stack = sb("q_stack", [P, BUFS, HG, UT], F16)
        k_stack = sb("k_stack", [P, BUFS, HG, HJ, UT], F16)
        v_ext = sb("v_ext", [P, BUFS, UW, HP, VC])
        g_hi = sb("g_hi", [P, BUFS, UW, 2, WIN], F16)
        g_lo = sb("g_lo", [P, BUFS, UW, 2, WIN], F16)
        w_hi = sb("w_hi", [P, 3, P], F16)
        w_lo = sb("w_lo", [P, 3, P], F16)
        pw = sb("pw", [P, 2, P])
        c_hi = sb("c_hi", [P, MATS, P], F16)
        c_lo = sb("c_lo", [P, MATS, P], F16)
        ident = sb("ident", [P, P])
        share = sb("share", [P, P])
        vecs = sb("vecs", [P, 4])
        st = sb("st", [P, UNITS, 6])
        sc = sb("sc", [P, 24])
        cf = sb("cf", [P, 12])
        am = sb("am", [P, 8])
        ws = sb("ws", [P, 8])
        m_all = sb("m_all", [P, 2, HG, PAIRS, HJ])
        m_pair = sb("m_pair", [PAIRS * HEADS, 2, P], F16)

        work = sb("work", [P, 8468])
        def part(at, n):
            return work[:, at:at + n]
        aff = part(0, 512)
        gpre = part(512, 512)
        g32 = part(1024, 512)
        qk = part(1536, 1024).bitcast(F16).rearrange("p (s t) -> p s t", s=4)
        probs = part(2580, 2 * 512).rearrange("p (s t) -> p s t", s=2)
        sums = [part(3604, 512), part(4116, 512)]
        guess = [part(4628, 512), part(5140, 512)]
        recip = [part(5652, 512), part(6164, 512)]
        res = part(6676, 512)
        o_n = part(7188, 1024).rearrange("p (w a q) -> p w a q", w=UW, a=2)
        cx = part(0, HALO * WIDE).rearrange("p (r c) -> p r c", r=HALO)
        plane = [part(1300 + i * 640, 640).rearrange("p (r c) -> p r c", r=HALO) for i in range(PLANES)]
        x_hi = part(3860, 1280).bitcast(F16).rearrange("p (i r c) -> p i r c", i=PLANES, r=HALO)
        x_lo = part(5140, 1280).bitcast(F16).rearrange("p (i r c) -> p i r c", i=PLANES, r=HALO)
        c_out = [part(6420 + i * 1024, 1024).rearrange("p (r c) -> p r c", r=CROWS) for i in range(2)]
        kept = [buf[:, 1:3, :, :, :].bitcast(F32).rearrange("p m w e q -> p (m w e q)").rearrange(
            "p (r c) -> p r c", r=CROWS) for buf in (g_hi, g_lo)]
        raw_qkv = part(0, 384).rearrange("p (t c) -> p t c", t=3)
        raw_proj = part(384, 256).rearrange("p (a c r) -> p a c r", a=2, c=4)
        raw_conv = part(640, C * TAPS).rearrange("p (i k) -> p i k", k=TAPS)
        mixed = part(1792, 2 * ROW_TAPS * C).rearrange("p (m k i) -> p m k i", m=2, k=ROW_TAPS)
        outer = part(2560, ROW_TAPS * C).rearrange("p (k i) -> p k i", k=ROW_TAPS)
        middle = part(2944, ROW_TAPS * C).rearrange("p (k i) -> p k i", k=ROW_TAPS)
        ones = work[0:2, 3328:3328 + P]

        ps = ctx.enter_context(nc.psum_tensor("ps", [P, 8, 512], F32))
        S_B, ST_B, PV_B, GA, GB = 0, 2, 4, 6, 7
        NORM = 0

        mask4 = sb("mask4", [P, HJ])
        names = {}
        def sem(name, per=1):
            s = ctx.enter_context(nc.semaphore(name))
            names[name] = (s, per)
            return s

        aff_done = sem("aff_done"); gpre_done = sem("gpre_done"); g32_done = sem("g32_done")
        g_hi_done = sem("g_hi_done", 2); g_lo_done = sem("g_lo_done", 2)
        q_done = sem("q_done"); k_done = sem("k_done"); v_done = sem("v_done", 2)
        q_hi_done = sem("q_hi_done"); q_lo_done = sem("q_lo_done")
        k_hi_done = sem("k_hi_done"); k_lo_done = sem("k_lo_done")
        v_out = sem("v_out", 4)
        q_sent = sem("q_sent", 32); k_sent = sem("k_sent", 32)
        q_in = sem("q_in", 32); k_in = sem("k_in", 64)
        s_done = sem("s_done", 8); max_done = sem("max_done", 8)
        mt_done = sem("mt_done"); m_hi_done = sem("m_hi_done"); m_lo_done = sem("m_lo_done")
        m_sent = sem("m_sent", 16); m_in = sem("m_in", 16)
        st_done = sem("st_done", 8); exp_done = sem("exp_done", 8); pv_done = sem("pv_done", 8)
        sums_done = sem("sums_done", 2); ln_done = sem("ln_done", 2); guess_done = sem("guess_done", 2)
        near_done = sem("near_done", 2); recip_done = sem("recip_done", 2); o_done = sem("o_done", 2)
        proj_done = sem("proj_done"); res_done = sem("res_done"); x1_done = sem("x1_done")
        bn_done = sem("bn_done")
        cx_done = sem("cx_done"); even_planes = sem("even_planes", 2); odd_planes = sem("odd_planes", 2)
        x_hi_done = sem("x_hi_done", PLANES); x_lo_done = sem("x_lo_done", PLANES)
        conv_done = sem("conv_done", PLANES); m0_out = sem("m0_out"); m1_out = sem("m1_out"); m2_out = sem("m2_out", 2)
        m3_out = sem("m3_out"); cadd_done = sem("cadd_done")
        out_done = sem("out_done", 16); next_in = sem("next_in", 16); nbn_done = sem("nbn_done")
        settled = sem("settled")
        zeros_out = sem("zeros_out"); w_in = sem("w_in"); x_in = [sem(f"x_in{i}") for i in range(LOADS)]; kept_done = sem("kept_done")
        pool_set = sem("pool_set"); pe_step = sem("pe_step"); act_step = sem("act_step")
        dve_step = sem("dve_step"); coef_ready = sem("coef_ready"); pads_zero = sem("pads_zero")
        aggr_done = sem("aggr_done"); gmean_done = sem("gmean_done"); dev_done = sem("dev_done")
        gvar_done = sem("gvar_done"); var_done = sem("var_done"); root_done = sem("root_done")
        amax_done = sem("amax_done"); diag_done = sem("diag_done"); scaled_done = sem("scaled_done")

        COUNTED = [n for n in names if n not in (
            "settled zeros_out w_in kept_done pool_set pe_step act_step dve_step coef_ready pads_zero "
            "amax_done diag_done scaled_done aggr_done gmean_done dev_done gvar_done var_done root_done".split()) and not n.startswith("x_in")]

        def after(eng, s, unit, k=None):
            name = next(n for n, (h, _) in names.items() if h is s)
            per = names[name][1]
            eng.wait_ge(s, unit * per + (AHEAD * per + (per if k is None else k)))
            if eng is nc.sync:
                settle(eng)

        def settle(eng):
            eng.sem_inc(settled, 1)

        def pixels(u):
            return (u // ACROSS) * WS, (u % ACROSS) * UCOL

        block = ctx.enter_context(nc.Block())

        def iterations(eng, b, one, late=None):
            def active(i):
                return {s for s, lead in (("G", 4), ("H", 3), ("B", 2), ("C", 1), ("D", 0), ("R", -1), ("X", -2))
                        if 0 <= i + lead < UNITS}
            first, turns = 2, (UNITS - 6) // BUFS
            for i in range(-4, first):
                if i == -2 and late:
                    late()
                one(i, i % BUFS, active(i))
            with eng.Fori(0, turns) as t:
                for k in range(BUFS):
                    one(t * BUFS + (first + k), (first + k) % BUFS, active(first))
            for i in range(first + turns * BUFS, UNITS + 2):
                one(i, i % BUFS, active(i))

        def conv_units(eng, b, one):
            one(0, 0, True, False)
            one(1, 1, False, False)
            with eng.Fori(0, (CUNITS - 4) // 2) as t:
                one(t * 2 + 2, 0, False, False)
                one(t * 2 + 3, 1, False, False)
            for t in range(CUNITS - 2, CUNITS):
                one(t, t % 2, False, t == CUNITS - 1)

        def key_major(row, by_window=False):
            if by_window:
                return row.rearrange("p (w k) -> p k w", w=UW)
            return row.rearrange("p (k w) -> p k w", w=UW)

        def peeled(i, k):
            return isinstance(i, int) and i == k

        def before_last(t):
            return 1 if peeled(t, CUNITS - 2) else 0

        def column(buf, s):
            return buf[:, :, s:s + SIDE - 1:2]

        def outputs(buf, s):
            return buf.rearrange("p r (c e) -> p (r c) e", e=2)[:, :, s]

        def v_heads(bank, parity):
            rows = slice(64 * parity, 64 * parity + 64)
            return ps[rows, bank, :].rearrange("p (w h e d) -> p w h e d", w=4, e=2, d=HD)[:, :, :, parity, :]

        A_SLOPE, A_OFF, A_MEAN, C_SLOPE, C_OFF = 0, 1, 2, 3, 4
        S_QKV, S_CONV, R_QKV, R_CONV, R_EXP, R_RES, R_MINUS = 0, 1, 2, 3, 4, 5, 6

        @block.sync
        def _(sp):
            sp.wait_ge(pool_set, 1)
            sp.dma_start(raw_qkv, qkv_w.rearrange("(t d) c -> d t c", t=3)).then_inc(w_in, 16)
            for a in range(2):
                sp.dma_start(raw_proj[:, a, :, 0:2 * HD], proj_w[:, a * 64:(a + 1) * 64].rearrange("o (c r) -> o c r", r=16)).then_inc(w_in, 16)
            sp.dma_start(raw_conv, conv_w.rearrange("o i h w -> o i (h w)")).then_inc(w_in, 16)
            for i, v in enumerate((ac_w, ac_b, proj_b)):
                sp.dma_start(vecs[:, i:i + 1], v.rearrange("(c a) -> c a", a=1)).then_inc(w_in, 16)
            sp.dma_start(vecs[:, 3:4], conv_b.rearrange("c a b -> c (a b)")).then_inc(w_in, 16)
            rows = SIDE // LOADS
            for i in range(LOADS):
                sp.dma_start(img[:, rows * i:rows * i + rows, :], x[0, :, rows * i:rows * i + rows, :]).then_inc(x_in[i], 16)
            sp.wait_ge(pool_set, 12)
            sp.dma_start(zerod, k_stack[0:MROWS, 0, :, 0, :]).then_inc(zeros_out, 16)
            sp.wait_ge(zeros_out, 16)
            sp.wait_ge(pool_set, 13)
            sp.wait_ge(act_step, 9)

            for b in range(BATCH):
                def one(i, m, on):
                    n = i + b * UNITS
                    if "B" in on:
                        d, mb = n + 2, (m + 2) % BUFS
                        n_r = HD * PARTS
                        k_rows = stackd[mb, 1].rearrange("(g j d) s t -> j (d s) g t", g=HG, j=HJ)
                        for which, lo, hi, into, sent in ((0, q_lo_done, q_hi_done, q_in, q_sent),
                                                          (1, k_lo_done, k_hi_done, k_in, k_sent)):
                            after(sp, into, d - 1)
                            after(sp, lo, d)
                            after(sp, hi, d)
                            to = stackd[mb, which]
                            sp.dma_start(to[:, 0:2, :], qk[:, 2 * which:2 * which + 2, :]).then_inc(sent, 16)
                            sp.dma_start(to[:, 2, :], qk[:, 1 + which, :]).then_inc(sent, 16)
                            if which == 0:
                                after(sp, st_done, d - BUFS)
                                sp.dma_start(q_stack[ROWS:ROWS + MROWS, mb, :, :], zerod).then_inc(q_in, 16)
                        after(sp, q_sent, d)
                        sp.dma_start(q_stack[0:ROWS, mb, :, :],
                                     stackd[mb, 0].rearrange("(g r) s t -> (r s) g t", g=HG)).then_inc(q_in, 16)
                        after(sp, k_sent, d)
                        for j in range(HJ):
                            sp.dma_start(k_stack[n_r * j:n_r * j + n_r, mb, :, j, :], k_rows[j]).then_inc(k_in, 16)
                    if "C" in on:
                        d, mb = n + 1, (m + 1) % BUFS
                        after(sp, m_in, d - 1)
                        after(sp, m_hi_done, d)
                        after(sp, m_lo_done, d)
                        sp.dma_start(maxd[mb], m_pair[:, :, :]).then_inc(m_sent, 16)
                        after(sp, m_sent, d)
                        after(sp, st_done, d - BUFS)
                        sp.dma_start(q_stack[ROWS:ROWS + MROWS, mb, :, :].rearrange("r g (p t) -> r (g p) t", p=PAIRS),
                                     maxd[mb].rearrange("(a j) s t -> (j s) a t", j=HJ)).then_inc(m_in, 16)
                iterations(sp, b, one)

                def store(t, par):
                    n = t + b * CUNITS
                    after(sp, cadd_done, n)
                    after(sp, out_done, n - 1)
                    sp.dma_start(out[b, :, bass.ds(t * CROWS, CROWS), :], c_out[par][:, :, :]).then_inc(out_done, 16)

                def conv_one(t, par, top, bottom):
                    n = t + b * CUNITS

                    def refill(s, event):
                        sp.dma_start(img[:, bass.ds(s * CROWS, CROWS), :],
                                     x[b + 1, :, bass.ds(s * CROWS, CROWS), :]).then_inc(event, 16)
                    if b + 1 < BATCH and peeled(t, CUNITS - 2):
                        after(sp, cx_done, n + 1)
                        sp.wait_ge(kept_done, 2)
                        for e in range(2):
                            refill(t + e, x_in[e])
                    if not top:
                        store(t - 1, 1 - par)
                    if b + 1 < BATCH and not top and not bottom:
                        after(sp, cx_done, n)
                        after(sp, next_in, t - 2)
                        refill(t - 1, next_in)
                    if bottom:
                        store(t, par)
                conv_units(sp, b, conv_one)
            after(sp, out_done, BATCH * CUNITS - 1)

        @block.gpsimd
        def _(pool):
            g = nc.gpsimd
            g.memset(raw_proj, 0.0).then_inc(pool_set, 1)
            pool.wait_ge(pool_set, 1)
            g.memset(ident[:, :], 0.0).then_inc(pool_set, 1)
            pool.wait_ge(pool_set, 2)
            g.memset(share[:, :], 1.0 / GC).then_inc(pool_set, 1)
            pool.wait_ge(pool_set, 3)
            g.memset(ones[:, :], 1.0).then_inc(pool_set, 1)
            pool.wait_ge(pool_set, 4)
            g.memset(mask4[ROWS:P, :], -PAIR_MAX).then_inc(pool_set, 1)
            pool.wait_ge(pool_set, 5)
            g.memset(m_all[:, 1, :, :, :], 0.0).then_inc(pool_set, 1)
            pool.wait_ge(pool_set, 6)
            g.affine_select(out=ident[:, :], in_=ident[:, :], compare_op=ALU.not_equal, fill=1.0,
                            base=0, pattern=[[-1, P]], channel_multiplier=1).then_inc(pool_set, 1)
            pool.wait_ge(pool_set, 7)
            sv = share[:, :].rearrange("p (a c) -> p a c", c=GC)
            g.affine_select(out=sv, in_=sv, compare_op=ALU.is_ge, fill=0.0,
                            base=0, pattern=[[-GC, GROUPS], [0, GC]], channel_multiplier=1).then_inc(pool_set, 1)
            pool.wait_ge(pool_set, 8)
            mv = mask4[ROWS:P, :]
            g.affine_select(out=mv, in_=mv, compare_op=ALU.is_ge, fill=0.0,
                            base=0, pattern=[[-2, HJ]], channel_multiplier=1).then_inc(pool_set, 1)
            pool.wait_ge(pool_set, 9)
            g.affine_select(out=sv, in_=sv, compare_op=ALU.is_ge, fill=0.0,
                            base=GC - 1, pattern=[[GC, GROUPS], [0, GC]], channel_multiplier=-1).then_inc(pool_set, 1)
            pool.wait_ge(pool_set, 10)
            g.affine_select(out=mv, in_=mv, compare_op=ALU.is_ge, fill=0.0,
                            base=1, pattern=[[2, HJ]], channel_multiplier=-1).then_inc(pool_set, 1)
            pool.wait_ge(pool_set, 11)
            g.memset(k_stack[:, :, :, :, :].bitcast(F32), 0.0).then_inc(pool_set, 1)
            pool.wait_ge(pool_set, 12)
            g.memset(q_stack[ROWS:P, :, :, :], 0.0).then_inc(pool_set, 1)
            pool.wait_ge(pool_set, 13)
            g.memset(v_ext[:, :, :, :, :], 0.0).then_inc(pool_set, 1)
            pool.wait_ge(pool_set, 14)
            ve = v_ext[:, :, :, :, :].rearrange("p m w h v -> p (m w h) v")
            g.memset(ve[0:64, :, 2 * HD:3 * HD], 1.0).then_inc(pool_set, 1)
            pool.wait_ge(pool_set, 15)
            g.memset(ve[64:P, :, 3 * HD:4 * HD], 1.0).then_inc(pool_set, 1)
            pool.wait_ge(pool_set, 16)

            for b in range(BATCH):
                def one(i, m, on):
                    n = i + b * UNITS

                    def nearness(d, h):
                        after(pool, guess_done, d, h + 1)
                        after(pool, o_done, d - 1, h + 1)
                        g.tensor_tensor(recip[h], sums[h], guess[h], ALU.mult).then_inc(near_done, 1)
                    if "R" in on:
                        nearness(n - 1, 1)
                    if "H" in on:
                        for e in range(2):
                            after(pool, g_hi_done, n + 3, e + 1)
                            g.tensor_tensor(g_lo[:, m, :, e, :], g32.rearrange("p (w q) -> p w q", w=UW),
                                            g_hi[:, m, :, e, :], ALU.subtract).then_inc(g_lo_done, 1)
                    if "D" in on:
                        nearness(n, 0)
                    if "R" in on:
                        row, col = pixels(i - 1)
                        here = img[:, bass.ds(row, WS), bass.ds(col, UCOL)]
                        after(pool, res_done, n - 1)
                        g.tensor_tensor(here, here, res.rearrange("p (r c) -> p r c", r=WS), ALU.add).then_inc(x1_done, 1)
                def last_unit():
                    residual(CUNITS - 1, b * CUNITS - 1, 1, kept[1])
                iterations(pool, b, one, late=last_unit if b else None)

                def residual(t, n, par, strip=None):
                    after(pool, m3_out, n)
                    after(pool, m2_out, n)
                    x1 = img[:, bass.ds(t * CROWS, CROWS), :] if strip is None else strip[:, :, :]
                    g.tensor_tensor(c_out[par][:, :, :], c_out[par][:, :, :], x1, ALU.add).then_inc(cadd_done, 1)

                def conv_one(t, par, top, bottom):
                    n = t + b * CUNITS
                    more = b + 1 < BATCH

                    def odd_plane(k, t, n):
                        after(pool, cx_done, n)
                        after(pool, x_lo_done, n - 1, 2 * k + 2)
                        if peeled(t, CUNITS - 1):
                            pool.wait_ge(pads_zero, 4 * b + 4)
                        c, op = ((2, ALU.add), (3, ALU.subtract))[k]
                        g.tensor_tensor(plane[2 * k + 1], column(cx, 1), column(cx, c), op).then_inc(odd_planes, 1)
                    if more and top:
                        after(pool, x1_done, (b + 1) * UNITS - 1)
                        after(pool, proj_done, (b + 1) * UNITS - 1)
                        for e in range(2):
                            r0 = (CUNITS - 2 + e) * CROWS
                            g.tensor_copy(kept[e][:, :, :], img[:, r0:r0 + CROWS, :]).then_inc(kept_done, 1)
                        pool.wait_ge(kept_done, 2)
                    if top:
                        pool.wait_ge(pads_zero, 4 * b + 3)
                        odd_plane(0, t, n)
                        odd_plane(1, t, n)
                    if not bottom:
                        odd_plane(0, t + 1, n + 1)
                    if not bottom:
                        odd_plane(1, t + 1, n + 1)
                    if not top:
                        residual(t - 1, n - 1, 1 - par, kept[0] if more and bottom else None)
                    if bottom and not more:
                        residual(t, n, par)
                conv_units(pool, b, conv_one)

        @block.scalar
        def _(act):
            a = nc.scalar
            for n in COUNTED:
                s, per = names[n]
                act.sem_inc(s, AHEAD * per)

            def root(k):
                act.wait_ge(var_done, k + 1)
                a.activation(sc[:, 5:6], sc[:, 4:5], ACT.Sqrt).then_inc(root_done, 1)

            act.wait_ge(pe_step, 3)
            a.copy(w_hi[:, :, :], ps[:, 0, 0:3 * P].rearrange("p (t d) -> p t d", t=3)).then_inc(act_step, 1)
            act.wait_ge(pe_step, 4)
            a.copy(pw[:, :, :], ps[:, 1, 0:2 * P].rearrange("p (t d) -> p t d", t=2)).then_inc(act_step, 1)
            for j in range(MATS // 4):
                act.wait_ge(pe_step, 5 + j)
                a.copy(c_hi[:, 4 * j:4 * j + 4, :], ps[:, 2 + j, :].rearrange("p (t d) -> p t d", d=P)).then_inc(act_step, 1)

            act.wait_ge(pool_set, 12)
            for j in range(HJ):
                rows = k_stack[ROWS:ROWS + MROWS, :, :, j, :].rearrange("p m g t -> p (m g) t")
                a.activation(rows, rows, ACT.Identity, bias=mask4[ROWS:ROWS + MROWS, j:j + 1]).then_inc(act_step, 1)

            for b in range(BATCH):
                root(2 * b)
                act.preload_act_table_set("natural_log_exp_and_others")

                def one(i, m, on):
                    n = i + b * UNITS

                    def exps(w):
                        after(act, st_done, n, w + 1)
                        after(act, pv_done, n, w - 1)
                        a.activation(probs[:, w % 2, :], ps[:, ST_B + w % 2, :], ACT.Exp,
                                     scale=ws[:, R_EXP:R_EXP + 1]).then_inc(exp_done, 1)

                    def guesses(d, h):
                        after(act, sums_done, d, h + 1)
                        a.activation(guess[h], sums[h], ACT.Ln).then_inc(ln_done, 1)
                        after(act, ln_done, d, h + 1)
                        a.activation(guess[h], guess[h], ACT.Exp, scale=-1.0).then_inc(guess_done, 1)

                    def v_copies(h):
                        mb = (m + 2) % BUFS
                        if peeled(i, -2) and b == 0 and h == 0:
                            act.wait_ge(pool_set, 16)
                        after(act, v_done, n + 2, h + 1)
                        after(act, pv_done, n + 2 - BUFS)
                        for parity in range(2):
                            a.copy(v_ext[64 * parity:64 * parity + 64, mb, 4 * h:4 * h + 4, :, HD * parity:HD * parity + HD],
                                   v_heads(GA + h, parity)).then_inc(v_out, 1)
                    if "B" in on:
                        after(act, q_done, n + 2)
                        after(act, q_sent, n + 1)
                        a.copy(qk[:, 1, :], ps[:, GA, :]).then_inc(q_hi_done, 1)
                    if "R" in on:
                        guesses(n - 1, 1)
                    if "B" in on:
                        after(act, k_done, n + 2)
                        after(act, k_sent, n + 1)
                        a.copy(key_major(qk[:, 2, :]), key_major(ps[:, GB, :], True)).then_inc(k_hi_done, 1)
                    if "D" in on:
                        exps(0)
                        exps(1)
                    if "B" in on:
                        v_copies(0)
                    if "D" in on:
                        exps(2)
                    if "D" in on:
                        exps(3)
                    if "H" in on:
                        after(act, g32_done, n + 3)
                        after(act, v_done, n)
                        if peeled(i, -2) and b:
                            after(act, cadd_done, b * CUNITS - 1)
                        for e in range(2):
                            a.copy(g_hi[:, m, :, e, :], g32.rearrange("p (w q) -> p w q", w=UW)).then_inc(g_hi_done, 1)
                    if "B" in on:
                        v_copies(1)
                    if "D" in on:
                        exps(4)
                    if "G" in on:
                        row, col = pixels(i + 4)
                        if peeled(i, -4):
                            act.wait_ge(coef_ready, 2 * b + 1)
                            after(act, x_lo_done, b * CUNITS - 1)
                        after(act, gpre_done, n + 3)
                        a.activation(aff.rearrange("p (r c) -> p r c", r=WS), img[:, bass.ds(row, WS), bass.ds(col, UCOL)],
                                     ACT.Identity, scale=cf[:, A_SLOPE:A_SLOPE + 1], bias=cf[:, A_OFF:A_OFF + 1]).then_inc(aff_done, 1)
                    if "D" in on:
                        exps(5)
                    if "C" in on:
                        after(act, mt_done, n + 1)
                        after(act, m_sent, n)
                        a.mul(m_pair[:, 0, :], ps[0:PAIRS * HEADS, GA, 0:P], 1.0 / PAIR_MAX).then_inc(m_hi_done, 1)
                    if "D" in on:
                        exps(6)
                        exps(7)
                        guesses(n, 0)
                    if "R" in on:
                        after(act, proj_done, n - 1)
                        after(act, x1_done, n - 2)
                        a.activation(res.rearrange("p (y n x) -> p n y x", y=WS, n=UW),
                                     ps[:, GB, :].rearrange("p (n y x) -> p n y x", y=WS, n=UW), ACT.Identity,
                                     scale=ws[:, R_RES:R_RES + 1], bias=vecs[:, 2:3]).then_inc(res_done, 1)
                iterations(act, b, one, late=(lambda: first_out(b * CUNITS - 1, 1)) if b else None)

                root(2 * b + 1)

                def first_out(n, par):
                    after(act, conv_done, n, 2)
                    after(act, out_done, n - 2)
                    a.activation(outputs(c_out[par], 1), ps[:, PLANES * par + 1, :], ACT.Identity,
                                 scale=ws[:, R_CONV:R_CONV + 1], bias=vecs[:, 3:4]).then_inc(m1_out, 1)

                def conv_one(t, par, top, bottom):
                    n = t + b * CUNITS

                    def normed(t, n, r0, r1):
                        after(act, even_planes, n - 1)
                        after(act, odd_planes, n - 1)
                        a.activation(cx[:, r0:r1, 1:1 + SIDE], img[:, bass.ds(t * CROWS - 1 + r0, r1 - r0), :],
                                     ACT.Identity, scale=cf[:, C_SLOPE:C_SLOPE + 1], bias=cf[:, C_OFF:C_OFF + 1]).then_inc(cx_done, 1)

                    def high(i, n):
                        after(act, (even_planes, odd_planes)[i % 2], n, i // 2 + 1)
                        after(act, conv_done, n - 1, i + 1)
                        a.copy(x_hi[:, i, :, :], plane[i]).then_inc(x_hi_done, 1)
                    if top:
                        act.wait_ge(coef_ready, 2 * b + 2)
                        normed(t, n, 1, HALO)
                        for i in range(PLANES - 1):
                            high(i, n)
                    if not bottom:
                        normed(t + 1, n + 1, 0, HALO - before_last(t))
                    high(3, n)
                    if not bottom:
                        high(0, n + 1)
                        high(1, n + 1)
                    if not bottom or b + 1 == BATCH:
                        first_out(n, par)
                    if not bottom:
                        high(2, n + 1)
                conv_units(act, b, conv_one)

        @block.vector
        def _(dve):
            v = nc.vector
            chain = [0]

            def link(ins):
                chain[0] += 1
                ins.then_inc(dve_step, 1)
                dve.wait_ge(dve_step, chain[0])

            dve.wait_ge(w_in, 16 * 8)
            v.tensor_reduce(am[:, 0:1], raw_qkv, AX.XY, ALU.max, apply_absolute_value=True).then_inc(amax_done, 1)
            v.tensor_reduce(am[:, 1:2], raw_conv, AX.XY, ALU.max, apply_absolute_value=True).then_inc(amax_done, 1)
            dve.wait_ge(pe_step, 1)
            link(v.tensor_reduce(am[0:2, 2:3], ps[0:2, 0, 0:P], AX.X, ALU.max))
            dve.wait_ge(pool_set, 7)
            v.tensor_scalar(am[0:2, 4:6], ident[0:2, 0:2], am[0:2, 2:3], None, ALU.mult).then_inc(diag_done, 1)
            dve.wait_ge(pe_step, 2)
            link(v.tensor_scalar(am[:, 6:8], ps[:, 0, 0:2], TINY, None, ALU.max))
            link(v.reciprocal(ws[:, 6:8], am[:, 6:8]))
            for col, src, f in ((S_QKV, ws[:, 6:7], QKV_SCALE), (S_CONV, ws[:, 7:8], CONV_SCALE),
                                (R_QKV, am[:, 6:7], 1.0 / QKV_SCALE), (R_CONV, am[:, 7:8], 1.0 / CONV_SCALE)):
                link(v.tensor_scalar(ws[:, col:col + 1], src, f, None, ALU.mult))
            link(v.tensor_scalar(ws[:, 5:6], ws[:, R_QKV:R_QKV + 1], HD ** -0.5, None, ALU.mult))
            link(v.tensor_tensor(ws[:, R_EXP:R_EXP + 1], ws[:, 5:6], ws[:, R_QKV:R_QKV + 1], ALU.mult))
            link(v.tensor_scalar(ws[:, R_RES:R_RES + 1], ws[:, R_QKV:R_QKV + 1], -1.0, None, ALU.mult))
            v.tensor_scalar(raw_qkv, raw_qkv, ws[:, S_QKV:S_QKV + 1], None, ALU.mult).then_inc(scaled_done, 1)
            link(v.tensor_scalar(ws[:, R_MINUS:R_MINUS + 1], ws[:, R_CONV:R_CONV + 1], -1.0, None, ALU.mult))
            link(v.tensor_scalar(raw_conv, raw_conv, ws[:, S_CONV:S_CONV + 1], None, ALU.mult))
            taps = [raw_conv[:, :, k:TAPS:3].rearrange("p i k -> p k i") for k in range(3)]
            link(v.tensor_scalar(middle, taps[1], 0.5, None, ALU.mult))
            link(v.tensor_tensor(outer, taps[0], taps[2], ALU.add))
            for e, op in enumerate((ALU.add, ALU.subtract)):
                link(v.scalar_tensor_tensor(out=mixed[:, e, :, :], in0=outer, scalar=0.5, in1=middle, op0=ALU.mult, op1=op))
            v.tensor_copy(am[:, 3:4], am[:, 0:1]).then_inc(scaled_done, 1)

            flat = img[:, :, :].rearrange("p r c -> p (r c)")
            for i in range(UNITS):
                if i % 4 == 0 and i <= 12:
                    if i == 0:
                        hi, lo, src = w_hi[:, :, :], w_lo[:, :, :], ps[:, 0, 0:3 * P]
                        dve.wait_ge(act_step, 1)
                    else:
                        j = i // 4 - 1
                        hi, lo, src = c_hi[:, 4 * j:4 * j + 4, :], c_lo[:, 4 * j:4 * j + 4, :], ps[:, 2 + j, :]
                        dve.wait_ge(act_step, 3 + j)
                    link(v.tensor_tensor(lo, src.rearrange("p (t d) -> p t d", d=P), hi, ALU.subtract))
                dve.wait_ge(x_in[i * LOADS // UNITS], 16)
                stats = v.bn_stats(st[:, i, :], flat[:, i * UT:(i + 1) * UT])
            link(stats)

            def norm(k):
                mean, var, gm, dev, gv, root, r, t0, t1 = (sc[:, j:j + 1] for j in (0, 1, 2, 3, 4, 5, 6, 7, 8))
                if k:
                    dve.wait_ge(root_done, k)
                v.bn_aggr(sc[:, 0:2], st[:, :, :].rearrange("p u s -> p (u s)")).then_inc(aggr_done, 1)
                dve.wait_ge(gmean_done, k + 1)
                link(v.tensor_copy(gm, ps[:, NORM, 0:1]))
                link(v.tensor_tensor(t0, mean, gm, ALU.subtract))
                link(v.tensor_tensor(t1, t0, t0, ALU.mult))
                v.tensor_tensor(dev, t1, var, ALU.add).then_inc(dev_done, 1)
                dve.wait_ge(gvar_done, k + 1)
                v.tensor_scalar(gv, ps[:, NORM, 1:2], EPS, None, ALU.add).then_inc(var_done, 1)
                dve.wait_ge(root_done, k + 1)
                link(v.reciprocal(r, root))
                link(v.tensor_tensor(t0, r, r, ALU.mult))
                link(v.tensor_tensor(t1, t0, gv, ALU.mult))
                link(v.tensor_scalar(t0, t1, -0.5, 1.5, ALU.mult, ALU.add))
                link(v.tensor_tensor(t1, r, t0, ALU.mult))
                link(v.tensor_copy(r, t1))
                return gm, r, t0, t1

            for b in range(BATCH):
                gm, r, t0, t1 = norm(2 * b)
                link(v.tensor_tensor(t0, r, vecs[:, 0:1], ALU.mult))
                link(v.tensor_tensor(t1, t0, gm, ALU.mult))
                link(v.tensor_tensor(sc[:, 9:10], vecs[:, 1:2], t1, ALU.subtract))
                link(v.tensor_tensor(cf[:, A_SLOPE:A_SLOPE + 1], t0, r, ALU.mult))
                link(v.tensor_tensor(cf[:, A_OFF:A_OFF + 1], sc[:, 9:10], r, ALU.mult))
                v.tensor_copy(cf[:, A_MEAN:A_MEAN + 1], gm).then_inc(coef_ready, 1)
                dve.wait_ge(coef_ready, 2 * b + 1)

                def one(i, m, on):
                    n = i + b * UNITS

                    def sum_rows(d, h):
                        after(dve, pv_done, d, 4 * h + 4)
                        after(dve, recip_done, d - 1, h + 1)
                        settle(dve)
                        v.stream_shuffle(sums[h], ps[:, PV_B + h, :], [16 + j % 16 for j in range(32)]).then_inc(sums_done, 1)

                    def divide(d, h):
                        after(dve, near_done, d, h + 1)
                        v.scalar_tensor_tensor(out=recip[h], in0=recip[h], scalar=-2.0, in1=guess[h],
                                               op0=ALU.add, op1=ALU.mult).then_inc(recip_done, 1)
                        after(dve, recip_done, d, h + 1)
                        after(dve, proj_done, d - 1)
                        v.tensor_tensor(o_n[:, 4 * h:4 * h + 4, :, :],
                                        ps[:, PV_B + h, :].rearrange("p (w a q) -> p w a q", w=4, a=2),
                                        recip[h].rearrange("p (w a q) -> p w a q", w=4, a=2), ALU.mult).then_inc(o_done, 1)

                    def row_max(p):
                        for h in range(2):
                            after(dve, s_done, n + 1, 2 * p + h + 1)
                            if p == 0 and h == 0:
                                after(dve, mt_done, n)
                            v.tensor_reduce(m_all[:, 0, 2 * h:2 * h + 2, p, :],
                                            ps[:, S_B + h, :].rearrange("p (g j k) -> p g j k", g=2, k=WIN), AX.X,
                                            ALU.max).then_inc(max_done, 1)
                    if peeled(i, 0) and b:
                        after(dve, out_done, b * CUNITS - 1)
                    if "R" in on:
                        sum_rows(n - 1, 1)
                    if "R" in on:
                        divide(n - 1, 0)
                    if "B" in on:
                        after(dve, q_hi_done, n + 2)
                        v.tensor_tensor(qk[:, 0, :], ps[:, GA, :], qk[:, 1, :], ALU.subtract).then_inc(q_lo_done, 1)
                    if "C" in on:
                        row_max(0)
                    if "B" in on:
                        after(dve, k_hi_done, n + 2)
                        v.tensor_tensor(key_major(qk[:, 3, :]), key_major(ps[:, GB, :], True), key_major(qk[:, 2, :]),
                                        ALU.subtract).then_inc(k_lo_done, 1)
                    if "C" in on:
                        row_max(1)
                    if "R" in on:
                        divide(n - 1, 1)
                    if "C" in on:
                        row_max(2)
                        row_max(3)
                    if "D" in on:
                        sum_rows(n, 0)
                    if "C" in on:
                        after(dve, m_hi_done, n + 1)
                        v.scalar_tensor_tensor(out=m_pair[:, 1, :], in0=ps[0:PAIRS * HEADS, GA, 0:P], scalar=1.0 / PAIR_MAX,
                                               in1=m_pair[:, 0, :], op0=ALU.mult, op1=ALU.subtract).then_inc(m_lo_done, 1)
                    if "X" in on:
                        row, col = pixels(i - 2)
                        after(dve, x1_done, n - 2)
                        v.bn_stats(st[:, bass.ds(i - 2, 1), :].rearrange("p a s -> p (a s)"),
                                   img[:, bass.ds(row, WS), bass.ds(col, UCOL)]).then_inc(bn_done, 1)
                    if "G" in on:
                        row, col = pixels(i + 4)
                        after(dve, aff_done, n + 4)
                        after(dve, g32_done, n + 3)
                        v.scalar_tensor_tensor(out=gpre.rearrange("p (r c) -> p r c", r=WS),
                                               in0=img[:, bass.ds(row, WS), bass.ds(col, UCOL)],
                                               scalar=cf[:, A_MEAN:A_MEAN + 1],
                                               in1=aff.rearrange("p (r c) -> p r c", r=WS),
                                               op0=ALU.subtract, op1=ALU.mult).then_inc(gpre_done, 1)
                        after(dve, gpre_done, n + 4)
                        after(dve, g_lo_done, n + 3)
                        v.tensor_scalar(g32.rearrange("p (n y x) -> p y n x", n=UW, y=WS),
                                        gpre.rearrange("p (y n x) -> p y n x", y=WS, n=UW),
                                        0.0, G_MAX, ALU.max, ALU.min).then_inc(g32_done, 1)
                iterations(dve, b, one, late=(lambda: outputs_of(b * CUNITS - 1, 1)) if b else None)
                after(dve, bn_done, (b + 1) * UNITS - 1)

                gm, r, t0, t1 = norm(2 * b + 1)
                link(v.tensor_copy(cf[:, C_SLOPE:C_SLOPE + 1], r))
                link(v.tensor_tensor(t0, gm, r, ALU.mult))
                v.tensor_scalar(cf[:, C_OFF:C_OFF + 1], t0, -1.0, None, ALU.mult).then_inc(coef_ready, 1)
                dve.wait_ge(coef_ready, 2 * b + 2)
                for side in (0, WIDE - 1):
                    v.memset(cx[:, :, side:side + 1], 0.0).then_inc(pads_zero, 1)
                v.memset(cx[:, 0, 1:1 + SIDE], 0.0).then_inc(pads_zero, 1)
                dve.wait_ge(pads_zero, 4 * b + 3)

                sums_of = ((0, 0, 1, R_CONV, m0_out), (2, 0, 0, R_CONV, m2_out), (2, 1, 1, R_MINUS, m2_out),
                           (3, 1, 1, R_MINUS, m3_out))

                def outputs_of(n, par, steps=(0, 1, 2, 3)):
                    for step in steps:
                        m, to, old, col, event = sums_of[step]
                        after(dve, (m1_out, m0_out, m0_out, m2_out)[step], n)
                        after(dve, conv_done, n, m + 1)
                        v.scalar_tensor_tensor(out=outputs(c_out[par], to), in0=ps[:, PLANES * par + m, :],
                                               scalar=ws[:, col:col + 1], in1=outputs(c_out[par], old),
                                               op0=ALU.mult, op1=ALU.add).then_inc(event, 1)

                def conv_one(t, par, top, bottom):
                    n = t + b * CUNITS

                    def even_plane(k, t, n):
                        after(dve, cx_done, n)
                        after(dve, x_lo_done, n - 1, 2 * k + 1)
                        if peeled(t, CUNITS - 1) and k == 0:
                            after(dve, odd_planes, n - 1)
                            after(dve, even_planes, n - 1)
                            v.memset(cx[:, HALO - 1, 1:1 + SIDE], 0.0).then_inc(pads_zero, 1)
                            dve.wait_ge(pads_zero, 4 * b + 4)
                        a, c = ((0, 2), (2, 1))[k]
                        v.tensor_tensor(plane[2 * k], column(cx, a), column(cx, c), ALU.subtract).then_inc(even_planes, 1)

                    def low(i, n):
                        after(dve, x_hi_done, n, i + 1)
                        v.tensor_tensor(x_lo[:, i, :, :], plane[i], x_hi[:, i, :, :], ALU.subtract).then_inc(x_lo_done, 1)

                    more = b + 1 < BATCH
                    if top:
                        even_plane(0, t, n)
                        even_plane(1, t, n)
                        for i in range(PLANES - 1):
                            low(i, n)
                    if not bottom:
                        even_plane(0, t + 1, n + 1)
                    low(3, n)
                    if more and bottom:
                        strip_stats(t - 1)
                        strip_stats(t)
                    if not bottom:
                        even_plane(1, t + 1, n + 1)
                    if not top:
                        outputs_of(n - 1, 1 - par, (0,))
                    if not bottom:
                        low(0, n + 1)
                    if not top:
                        outputs_of(n - 1, 1 - par, (1, 2))
                    if not bottom:
                        low(1, n + 1)
                    if not top:
                        outputs_of(n - 1, 1 - par, (3,))
                    if not bottom:
                        low(2, n + 1)
                    if more and not top and not peeled(t, 1):
                        strip_stats(t - 2)
                    if bottom and not more:
                        outputs_of(n, par)

                def strip_stats(s):
                    if isinstance(s, int) and s >= CUNITS - 2:
                        dve.wait_ge(x_in[s - (CUNITS - 2)], 32)
                    else:
                        after(dve, next_in, s)
                    for half in range(2):
                        stats = v.bn_stats(st[:, bass.ds(s * 2 + half, 1), :].rearrange("p a s -> p (a s)"),
                                          img[:, bass.ds(s * CROWS + half * 4, 4), :])
                    stats.then_inc(nbn_done, 1)
                conv_units(dve, b, conv_one)
                if b + 1 < BATCH:
                    after(dve, nbn_done, CUNITS - 1)

        @block.tensor
        def _(pe):
            t_ = nc.tensor
            pe.wait_ge(pool_set, 11)
            pe.wait_ge(amax_done, 2)
            t_.transpose(ps[0:2, 0, 0:P], am[:, 0:2], ident[:, :]).then_inc(pe_step, 1)
            pe.wait_ge(diag_done, 1)
            t_.matmul(ps[:, 0, 0:2], ones[:, :], am[0:2, 4:6], start=True, stop=True).then_inc(pe_step, 1)
            pe.wait_ge(scaled_done, 1)
            for k in range(3):
                mm = t_.transpose(ps[:, 0, k * P:(k + 1) * P], raw_qkv[:, k, :], ident[:, :])
            mm.then_inc(pe_step, 1)
            for k in range(2):
                mm = t_.transpose(ps[:, 1, k * P:(k + 1) * P], raw_proj[:, k, :, :].rearrange("p c r -> p (c r)"), ident[:, :])
            mm.then_inc(pe_step, 1)
            pe.wait_ge(scaled_done, 2)
            for q in range(MATS):
                i, k = divmod(q, ROW_TAPS)
                src = mixed[:, i - 1, k, :] if i in (1, 2) else raw_conv[:, :, 3 * k + (0 if i == 0 else 2)]
                mm = t_.transpose(ps[:, 2 + q // 4, (q % 4) * P:(q % 4 + 1) * P], src, ident[:, :])
                if q % 4 == 3:
                    mm.then_inc(pe_step, 1)

            def norm_mean(k):
                pe.wait_ge(aggr_done, k + 1)
                t_.matmul(ps[:, NORM, 0:1], share[:, :], sc[:, 0:1], start=True, stop=True).then_inc(gmean_done, 1)

            def norm_variance(k):
                pe.wait_ge(dev_done, k + 1)
                t_.matmul(ps[:, NORM, 1:2], share[:, :], sc[:, 3:4], start=True, stop=True).then_inc(gvar_done, 1)

            def three(o, lhs_hi, lhs_lo, rhs_hi, rhs_lo, first=True, last=True):
                t_.matmul(o, lhs_hi, rhs_hi, start=first, stop=False)
                t_.matmul(o, lhs_lo, rhs_hi, start=False, stop=False)
                return t_.matmul(o, lhs_hi, rhs_lo, start=False, stop=last)

            norm_mean(0)
            norm_variance(0)
            for b in range(BATCH):
                def one(i, m, on):
                    n = i + b * UNITS

                    def project(which, bank, event):
                        mb = (m + 2) % BUFS
                        three(ps[:, bank, :], w_hi[:, which, :], w_lo[:, which, :],
                              g_hi[:, mb, :, 0, :], g_lo[:, mb, :, 0, :]).then_inc(event, 1)

                    def v_rows(h):
                        if h == 0:
                            after(pe, g_lo_done, n + 2)
                        mb = (m + 2) % BUFS
                        bank = GA + h
                        if h == 0:
                            after(pe, q_lo_done, n + 2)
                        else:
                            after(pe, k_lo_done, n + 2)
                        for w in range(4 * h, 4 * h + 4):
                            twice = [g[:, mb, w, :, :].rearrange("p e q -> p (e q)") for g in (g_hi, g_lo)]
                            o = ps[:, bank, (w % 4) * P:(w % 4 + 1) * P]
                            mm = three(o, twice[0], twice[1], w_hi[:, 2, :], w_lo[:, 2, :])
                        mm.then_inc(v_done, 1)

                    def keys(buf, g, j0, j1, w):
                        return k_stack[:, buf, g, j0:j1, :].rearrange("p j (k n) -> p (j k) n", n=UW)[:, :, w]

                    def scores(p):
                        mb = (m + 1) % BUFS
                        for h in range(2):
                            after(pe, max_done, n + 1, 2 * p + h - 1)
                            for gg in range(2):
                                for w in range(2):
                                    win = 2 * p + w
                                    tok = slice(win * WIN, (win + 1) * WIN)
                                    mm = t_.matmul(ps[64 * w:64 * w + 64, S_B + h, gg * 256:gg * 256 + 256],
                                                   q_stack[:, mb, 2 * h + gg, tok],
                                                   keys(mb, 2 * h + gg, 0, HJ, win), start=True, stop=True)
                            mm.then_inc(s_done, 1)

                    def scores_t(w):
                        tok = slice(w * WIN, (w + 1) * WIN)
                        after(pe, exp_done, n, w - 1)
                        for hp in range(HP):
                            g, j = hp // 2, 2 * (hp % 2)
                            mm = t_.matmul(ps[:, ST_B + w % 2, hp * WIN:(hp + 1) * WIN],
                                           keys(m, g, j, j + 2, w),
                                           q_stack[:, m, g, tok], start=True, stop=True)
                        mm.then_inc(st_done, 1)

                    def weigh(w):
                        after(pe, exp_done, n, w + 1)
                        if w % 4 == 0:
                            after(pe, o_done, n - 1, w // 4 + 1)
                        for hp in range(HP):
                            a, c = hp // 4, hp % 4
                            col = (w % 4) * P + a * WIN
                            mm = t_.matmul(ps[32 * c:32 * c + 32, PV_B + w // 4, col:col + WIN],
                                           v_ext[:, m, w, hp, :], probs[:, w % 2, hp * WIN:(hp + 1) * WIN],
                                           start=True, stop=True)
                        mm.then_inc(pv_done, 1)

                    def output(d):
                        after(pe, o_done, d)
                        for a in range(2):
                            mm = t_.matmul(ps[:, GB, :], pw[:, a, :], o_n[:, :, a, :], start=(a == 0), stop=(a == 1))
                        mm.then_inc(proj_done, 1)

                    if "B" in on:
                        after(pe, g_lo_done, n + 2, 1)
                        after(pe, m_lo_done, n)
                        after(pe, v_out, n + 1)
                        if peeled(i, -2) and b:
                            after(pe, m3_out, b * CUNITS - 1)
                        project(0, GA, q_done)
                    if "C" in on:
                        after(pe, q_in, n + 1)
                        after(pe, k_in, n + 1)
                        scores(0)
                    if "B" in on:
                        after(pe, res_done, n - 2)
                        project(1, GB, k_done)
                    if "D" in on:
                        after(pe, m_in, n)
                        scores_t(0)
                        scores_t(1)
                    if "B" in on:
                        v_rows(0)
                    if "C" in on:
                        scores(1)
                    if "D" in on:
                        scores_t(2)
                        weigh(0)
                        scores_t(3)
                        weigh(1)
                    if "B" in on:
                        v_rows(1)
                    if "C" in on:
                        scores(2)
                    if "D" in on:
                        weigh(2)
                        scores_t(4)
                        weigh(3)
                    if "C" in on:
                        scores(3)
                    if "D" in on:
                        scores_t(5)
                        weigh(4)
                        scores_t(6)
                    if "C" in on:
                        after(pe, max_done, n + 1)
                        if "B" in on:
                            after(pe, v_out, n + 2, 2)
                        t_.transpose(ps[:, GA, 0:P], m_all[:, :, :, :, :].rearrange("p e g a j -> p (e g a j)"),
                                     ident[:, :]).then_inc(mt_done, 1)
                    if "D" in on:
                        weigh(5)
                        scores_t(7)
                    if "R" in on:
                        if "B" in on:
                            after(pe, v_out, n + 2)
                        output(n - 1)
                    if "D" in on:
                        weigh(6)
                        weigh(7)
                iterations(pe, b, one)

                norm_mean(2 * b + 1)
                norm_variance(2 * b + 1)

                def conv_one(t, par, top, bottom):
                    n = t + b * CUNITS
                    for i in range(PLANES):
                        bank = PLANES * par + i
                        after(pe, x_lo_done, n, i + 1)
                        after(pe, (m0_out, m1_out, m2_out, m3_out)[i], n - 2)
                        for k in range(ROW_TAPS):
                            q = i * ROW_TAPS + k
                            mm = three(ps[:, bank, :], c_hi[:, q, :], c_lo[:, q, :],
                                       x_hi[:, i, k:k + CROWS, :], x_lo[:, i, k:k + CROWS, :],
                                       first=(k == 0), last=(k == ROW_TAPS - 1))
                        mm.then_inc(conv_done, 1)
                    if bottom and b + 1 < BATCH:
                        after(pe, m3_out, n - 1)
                        norm_mean(2 * b + 2)
                        norm_variance(2 * b + 2)
                conv_units(pe, b, conv_one)


_INS = ["x", "L0_conv_ac_w", "L0_conv_ac_b", "L0_conv_qkv_w", "L0_conv_proj_w", "L0_conv_proj_b",
        "L1_conv_W", "L1_conv_bias"]
_OUT = ((2, 128, 128, 128), "float32")


def kernel(**inputs):
    import numpy as _np
    import concourse.bacc as _bacc
    from concourse import mybir as _mybir
    from concourse.bass_utils import run_bass_kernel_spmd as _run

    nc = _bacc.Bacc("TRN2", target_bir_lowering=False, num_devices=1)
    arrays, args = {}, []
    for name in _INS:
        a = _np.ascontiguousarray(inputs[name])
        arrays[f"in_{name}_dram"] = a
        args.append(nc.dram_tensor(f"in_{name}_dram", a.shape, _mybir.dt.from_np(a.dtype), kind="ExternalInput").ap())
    shape, dtype = _OUT
    args.append(nc.dram_tensor("out_0_dram", shape, _mybir.dt.from_np(_np.dtype(dtype)), kind="ExternalOutput").ap())
    build(nc, *args)
    r = _run(nc, [arrays], core_ids=[0])
    return r.results[0]["out_0_dram"]
```
